# Optimizing a Trainium2 kernel written in Bass

```python
import numpy as np
import jax
import jax.numpy as jnp

def _softmax(x, axis=-1):
    return jax.nn.softmax(x, axis=axis)

def _gelu(x):
    return jax.nn.gelu(x, approximate=True)

def _silu(x):
    return jax.nn.silu(x)

def _sigmoid(x):
    return jax.nn.sigmoid(x)

def _layernorm(x, axis=-1, eps=1e-05):
    m = jnp.mean(x, axis=axis, keepdims=True)
    v = jnp.var(x, axis=axis, keepdims=True)
    return (x - m) / jnp.sqrt(v + eps)

def _scatter_add(tgt, idx, src, axis=0):
    return tgt.at[idx].add(src)

def _segment_sum(src, seg, n):
    return jax.ops.segment_sum(src, seg, n)
kernel_name = 'mk_early_fusion_d1_tok_img768_r4_6bb785'

def setup_inputs(seed: int=0):
    np.random.seed(seed)
    _w = jnp.asarray

    def _rec_inputs():
        import jax
        import jax.numpy as jnp
        _rk = jax.random.key(seed)
        x = 7.57192e-06 + 1.00007 * jax.random.normal(jax.random.fold_in(_rk, 1), (64, 224, 224, 3), jnp.float32)
        txt = -0.000292895 + 0.762493 * jax.random.normal(jax.random.fold_in(_rk, 2), (64, 32, 192), jnp.float32)
        return (x, txt)
    x, txt = _rec_inputs()

    def _L0_tok_setup():
        import jax, jax.numpy as jnp
        import numpy as np
        PATCH, OV, GRID, IMG = (16, 3, 14, 224)
        WIN = PATCH + 2 * OV

        def _window_index():
            starts = np.clip(np.arange(GRID) * PATCH - OV, 0, IMG - WIN)
            return (starts[:, None] + np.arange(WIN)[None, :]).reshape(-1)
        key = jax.random.key(seed)
        k1, k2 = jax.random.split(key)
        x = jax.random.normal(k1, (64, IMG, IMG, 3), dtype=jnp.float32)
        W = jax.random.normal(k2, (WIN * WIN * 3, 192), dtype=jnp.float32) * 0.02
        return {'x': x, 'W': W}
    _L0_tok_all = _L0_tok_setup()
    _L0_tok_in = {k: v for k, v in _L0_tok_all.items() if k in ('W',)}
    del _L0_tok_all

    def _L0_attn_setup():
        import jax, jax.numpy as jnp
        import numpy as np
        NUM_HEADS = 12
        NUM_PROMPT = 7
        NUM_PATCH = 4
        key = jax.random.key(seed)
        k1, k2, k3 = jax.random.split(key, 3)
        B, N, C = (4, 786, 192)
        x = jax.random.normal(k1, (B, N, C), dtype=jnp.float32)
        Wqkv = jax.random.normal(k2, (C, 3 * C), dtype=jnp.float32) * C ** (-0.5)
        Wproj = jax.random.normal(k3, (C, C), dtype=jnp.float32) * C ** (-0.5)
        bproj = jnp.zeros((C,), dtype=jnp.float32)
        return {'x': x, 'Wqkv': Wqkv, 'Wproj': Wproj, 'bproj': bproj}
    _L0_attn_all = _L0_attn_setup()
    _L0_attn_in = {k: v for k, v in _L0_attn_all.items() if k in ('Wqkv', 'Wproj', 'bproj')}
    del _L0_attn_all

    def _L0_ffn_setup():
        import jax, jax.numpy as jnp
        import numpy as np
        B, T, C = (4, 512, 192)
        E, K = (8, 2)

        def _mlp(x, wfc, wproj):
            h = jnp.square(jax.nn.relu(x @ wfc))
            return h @ wproj
        key = jax.random.key(seed)
        ks = jax.random.split(key, 6)
        s = 0.02
        return {'x': jax.random.normal(ks[0], (B, T, C), jnp.float32), 'w_fc_sh': jax.random.normal(ks[1], (C, C), jnp.float32) * s, 'w_proj_sh': jax.random.normal(ks[2], (C, C), jnp.float32) * s, 'w1': jax.random.normal(ks[3], (E, C, C), jnp.float32) * s, 'w2': jax.random.normal(ks[4], (E, C, C), jnp.float32) * s, 'router_w': jax.random.normal(ks[5], (E, C), jnp.float32) * s, 'balance_bias': jnp.zeros((E,), jnp.float32)}
    _L0_ffn_all = _L0_ffn_setup()
    _L0_ffn_in = {k: v for k, v in _L0_ffn_all.items() if k in ('w_fc_sh', 'w_proj_sh', 'w1', 'w2', 'router_w', 'balance_bias')}
    del _L0_ffn_all
    return {'x': x, 'txt': txt, 'L0_tok_W': _L0_tok_in['W'], 'L0_attn_Wqkv': _L0_attn_in['Wqkv'], 'L0_attn_Wproj': _L0_attn_in['Wproj'], 'L0_attn_bproj': _L0_attn_in['bproj'], 'L0_ffn_w_fc_sh': _L0_ffn_in['w_fc_sh'], 'L0_ffn_w_proj_sh': _L0_ffn_in['w_proj_sh'], 'L0_ffn_w1': _L0_ffn_in['w1'], 'L0_ffn_w2': _L0_ffn_in['w2'], 'L0_ffn_router_w': _L0_ffn_in['router_w'], 'L0_ffn_balance_bias': _L0_ffn_in['balance_bias']}

def reference(x, txt, L0_tok_W, L0_attn_Wqkv, L0_attn_Wproj, L0_attn_bproj, L0_ffn_w_fc_sh, L0_ffn_w_proj_sh, L0_ffn_w1, L0_ffn_w2, L0_ffn_router_w, L0_ffn_balance_bias):
    import jax
    import jax.numpy as jnp

    def _L0_tok_ref(x, W):
        import jax, jax.numpy as jnp
        import numpy as np
        PATCH, OV, GRID, IMG = (16, 3, 14, 224)
        WIN = PATCH + 2 * OV

        def _window_index():
            starts = np.clip(np.arange(GRID) * PATCH - OV, 0, IMG - WIN)
            return (starts[:, None] + np.arange(WIN)[None, :]).reshape(-1)
        B, _, _, C = x.shape
        idx = _window_index()
        g = jnp.take(x, idx, axis=1).reshape(B, GRID, WIN, IMG, C)
        g = jnp.take(g, idx, axis=3).reshape(B, GRID, WIN, GRID, WIN, C)
        patches = g.transpose(0, 1, 3, 2, 4, 5).reshape(B, GRID * GRID, WIN * WIN * C)
        return jnp.einsum('bnf,fd->bnd', patches, W)

    def _L0_attn_ref(x, Wqkv, Wproj, bproj):
        import jax, jax.numpy as jnp
        import numpy as np
        NUM_HEADS = 12
        NUM_PROMPT = 7
        NUM_PATCH = 4
        B, N, C = x.shape
        H = NUM_HEADS
        hd = C // H
        A = 1 + NUM_PROMPT
        P = NUM_PATCH
        inner = (N - A) // P
        scale = hd ** (-0.5)
        qkv = (x @ Wqkv).reshape(B, N, 3, H, hd)
        q, k, v = (qkv[:, :, 0], qkv[:, :, 1], qkv[:, :, 2])

        def split_tokens(t):
            aux = jnp.broadcast_to(t[:, None, :A].transpose(0, 1, 3, 2, 4), (B, P, H, A, hd))
            img = t[:, A:].reshape(B, inner, P, H, hd).transpose(0, 2, 3, 1, 4)
            return jnp.concatenate([aux, img], axis=3)
        qf = split_tokens(q) * scale
        kf = split_tokens(k)
        vf = split_tokens(v)
        attn = jnp.einsum('bphqd,bphkd->bphqk', qf, kf)
        attn = jax.nn.softmax(attn, axis=-1)
        out = jnp.einsum('bphqk,bphkd->bphqd', attn, vf)
        out = out.transpose(0, 1, 3, 2, 4).reshape(B, P, A + inner, C)
        aux_out = out[:, :, :A].mean(axis=1)
        img_out = out[:, :, A:].transpose(0, 2, 1, 3).reshape(B, N - A, C)
        y = jnp.concatenate([aux_out, img_out], axis=1)
        return y @ Wproj + bproj

    def _L0_ffn_ref(x, w_fc_sh, w_proj_sh, w1, w2, router_w, balance_bias):
        import jax, jax.numpy as jnp
        import numpy as np
        B, T, C = (4, 512, 192)
        E, K = (8, 2)

        def _mlp(x, wfc, wproj):
            h = jnp.square(jax.nn.relu(x @ wfc))
            return h @ wproj
        Bx, Tx, Cx = x.shape
        shared = _mlp(x, w_fc_sh, w_proj_sh)
        xf = x.reshape(-1, Cx)
        logits = xf.astype(jnp.float32) @ router_w.T
        scores = jax.nn.sigmoid(logits)
        _, idx = jax.lax.top_k(scores + balance_bias, K)
        tw = jnp.take_along_axis(scores, idx, axis=-1)
        tw = tw / (tw.sum(-1, keepdims=True) + 1e-20)
        combine = (jax.nn.one_hot(idx, E, dtype=tw.dtype) * tw[..., None]).sum(1)
        h = jnp.square(jax.nn.relu(jnp.einsum('nc,ech->neh', xf, w1)))
        y = jnp.einsum('neh,ehc->nec', h, w2)
        routed = jnp.einsum('nec,ne->nc', y, combine)
        return shared + routed.reshape(Bx, Tx, Cx)
    h = _L0_tok_ref(x, L0_tok_W)
    h = jnp.concatenate([h, txt], axis=1)
    h = h + _L0_attn_ref(_layernorm(h, axis=-1), L0_attn_Wqkv, L0_attn_Wproj, L0_attn_bproj)
    h = h + _L0_ffn_ref(_layernorm(h, axis=-1), L0_ffn_w_fc_sh, L0_ffn_w_proj_sh, L0_ffn_w1, L0_ffn_w2, L0_ffn_router_w, L0_ffn_balance_bias)
    return h

_drawn_inputs = setup_inputs


def setup_inputs(seed=0):
    import zlib

    import numpy as np

    out = dict(_drawn_inputs(seed))
    spreads = {'L0_attn_bproj': (0.0, 0.1), 'L0_ffn_balance_bias': (0.0, 0.344)}
    factors = {'L0_ffn_w1': 2.69, 'L0_ffn_router_w': 4.032}
    for name, (base, spread) in spreads.items():
        noise = np.random.default_rng([zlib.crc32(name.encode()), seed]).standard_normal(out[name].shape)
        drawn = base * np.exp(spread * noise) if base else spread * noise
        out[name] = jnp.asarray(drawn.astype(out[name].dtype))
    for name, factor in factors.items():
        out[name] = (out[name] * factor).astype(out[name].dtype)
    return out
```

```python
import numpy as np
import concourse.bass as bass
from concourse import mybir
from concourse.alu_op_type import AluOpType as ALU
from contextlib import ExitStack

F32 = mybir.dt.float32
ACT = mybir.ActivationFunctionType
AXX = mybir.AxisListType.X

GRID, IMG, WIN, PATCH, OVERLAP = 14, 224, 22, 16, 3
CH = 192
KC = 96
HEADS, HD = 12, 16
AUX, GROUPS = 8, 4
EPS = 1e-5


def wait(eng, sem, value):
    if isinstance(value, int) and value <= 0:
        return
    eng.wait_ge(sem, value)


def make_identity(nc, ident, n, zeroed, ready):
    nc.gpsimd.memset(ident, 0.0).then_inc(zeroed, 1)
    nc.gpsimd.wait_ge(zeroed, 1)
    nc.gpsimd.affine_select(out=ident, in_=ident, compare_op=ALU.not_equal, fill=1.0, base=0,
                            pattern=[[-1, n]], channel_multiplier=1).then_inc(ready, 1)


def embed_patches(nc, patches, w_tok, h_img):
    chunks, kp, kt, m = patches.shape
    RING = 7
    rounds = chunks // RING
    assert chunks == rounds * RING and m == 128
    with ExitStack() as ctx:
        sb = lambda name, shape: ctx.enter_context(nc.sbuf_tensor(name, shape, F32))
        sem = lambda name: ctx.enter_context(nc.semaphore(name))
        w = sb("w_tok_sb", [kp, kt, CH])
        pat = [sb(f"pat{i}", [kp, kt, m]) for i in range(RING)]
        emb = [sb(f"emb{i}", [m, CH]) for i in range(RING)]
        ps = [ctx.enter_context(nc.psum_tensor(f"emb_ps{i}", [m, CH], F32)) for i in range(RING)]
        w_in = sem("w_tok_in")
        pat_in = [sem(f"pat_in{i}") for i in range(RING)]
        emb_out = [sem(f"emb_out{i}") for i in range(RING)]
        emb_mm, emb_ev = sem("emb_mm"), sem("emb_ev")
        block = ctx.enter_context(nc.Block())

        @block.sync
        def _(sp):
            def load(k, i):
                sp.dma_start(pat[i][:, :, :], patches[k * RING + i, :, :, :]).then_inc(pat_in[i], 16)
            sp.dma_start(w[:, :, :], w_tok.rearrange("(t p) c -> p t c", p=kp)).then_inc(w_in, 16)
            for i in range(RING):
                load(0, i)
            with sp.Fori(1, rounds) as k:
                for i in range(RING):
                    sp.wait_ge(emb_mm, (k - 1) * RING + i + 1)
                    load(k, i)

        @block.tensor
        def _(pe):
            def tile(k, i):
                pe.wait_ge(pat_in[i], 16 * k + 16)
                wait(pe, emb_ev, k * RING + i + 1 - RING)
                for t in range(kt):
                    last = pe.matmul(ps[i][:, :], pat[i][:, t, :], w[:, t, :], start=(t == 0), stop=(t == kt - 1))
                last.then_inc(emb_mm, 1)
            pe.wait_ge(w_in, 16)
            for i in range(RING):
                tile(0, i)
            with pe.Fori(1, rounds) as k:
                for i in range(RING):
                    tile(k, i)

        @block.vector
        def _(dve):
            def tile(k, i):
                dve.wait_ge(emb_mm, k * RING + i + 1)
                wait(dve, emb_out[i], 16 * k)
                dve.tensor_copy(emb[i][:, :], ps[i][:, :]).then_inc(emb_ev, 1)
            for i in range(RING):
                tile(0, i)
            with dve.Fori(1, rounds) as k:
                for i in range(RING):
                    tile(k, i)

        @block.scalar
        def _(act):
            def store(k, i):
                act.wait_ge(emb_ev, k * RING + i + 1)
                act.dma_start(h_img[bass.ds((k * RING + i) * m, m), :], emb[i][:, :]).then_inc(emb_out[i], 16)
            with act.Fori(0, rounds) as k:
                for i in range(RING):
                    store(k, i)
            for i in range(RING):
                act.wait_ge(emb_out[i], 16 * rounds)


def attention(nc, h_img, txt, w_qkv, w_proj, b_proj, h1_out, x2_out):
    B, n_txt = txt.shape[0], txt.shape[1]
    n_img = h_img.shape[0] // B
    N = n_img + n_txt
    HT = N // 2
    INNER = (N - AUX) // GROUPS
    KEYS = AUX + INNER
    SL = 64
    HC = KC // HD
    PAIRS = HEADS // 2
    VW = 48
    assert B % 4 == 0 and 2 * HT == N and KEYS == SL - 1
    with ExitStack() as ctx:
        sb = lambda name, shape: ctx.enter_context(nc.sbuf_tensor(name, shape, F32))
        sem = lambda name: ctx.enter_context(nc.semaphore(name))
        pb = lambda name, shape: ctx.enter_context(nc.psum_tensor(name, shape, F32))
        ident = sb("ident_a", [128, 128])
        wqkv = sb("wqkv_sb", [KC, 2, 3 * CH])
        wproj = sb("wproj_sb", [KC + 1, 2, CH])
        mask = sb("head_mask", [KC, HC])
        h = [sb(f"h_sb{i}", [HT, 2, CH]) for i in range(4)]
        stats, mv = sb("stats", [HT, 2, 6]), sb("mv", [HT, 2, 2])
        vare, rstd = sb("vare", [HT, 2]), sb("rstd", [HT, 2])
        stats2, mv2 = sb("stats2", [HT, 2, 6]), sb("mv2", [HT, 2, 2])
        vare2, rstd2 = sb("vare2", [HT, 2]), sb("rstd2", [HT, 2])
        mhalf, eps = sb("minus_half", [HT, 2]), sb("eps", [HT, 2])
        carrier = sb("carrier", [HT, 1])
        xn = sb("xn", [HT, 2, CH])
        xT = sb("xT", [KC, 2, GROUPS, SL])
        qT = sb("qT", [KC, 2, GROUPS * SL])
        kT = sb("kT", [KC, 2 * GROUPS, SL])
        kbd = sb("kbd", [KC, 2 * GROUPS, HC, SL])
        vbd = [sb(f"vbd{i}", [128, 2, PAIRS, 2, VW]) for i in range(2)]
        prob = [sb(f"prob{t}", [128, HEADS, SL]) for t in range(2)]
        rmax = sb("rowmax", [128, 2, HEADS])
        pT = [sb(f"pT{t}", [128, PAIRS, 128]) for t in range(2)]
        rden = sb("rden", [128, 2, PAIRS, 2])
        o = sb("o", [128, 2, CH])
        oT = sb("oT", [KC + 1, 2, N])
        auxp = sb("auxp", [KC, 2, GROUPS, AUX])
        auxs = sb("auxs", [KC, 2, AUX])
        h1 = [sb(f"h1_{i}", [HT, 2, CH]) for i in range(2)]
        x2 = [sb(f"x2_{i}", [HT, 2, CH]) for i in range(2)]
        sc = [pb(f"sc{t}", [128, 2, 512]) for t in range(2)]
        px = pb("px", [128, 512])
        pw = pb("pw", [128, 512])
        pyz = pb("pyz", [128, 8, 128])
        x_v = px[0:KC, 0:2 * N].rearrange("p (c n) -> p c n", c=2)
        q_v = px[0:KC, :]
        v_v = px[:, 0:2 * CH].rearrange("p (t c) -> p t c", t=2)
        ot_v = px[0:KC, :].rearrange("p (c n) -> p c n", c=2)
        k_v = pw[0:KC, :]
        pr_v = pw[0:HT, 0:2 * CH].rearrange("p (t c) -> p t c", t=2)

        zeroed, consts, const_in = sem("zeroed_a"), sem("consts_a"), sem("const_in")
        values_zeroed, ones_set = sem("values_zeroed"), sem("ones_set")
        h_in = [sem(f"h_in{i}") for i in range(4)]
        ln_stats, ln_mv, ln_var, ln_rstd, xn_ready = (sem(n) for n in ("ln_stats", "ln_mv", "ln_var", "ln_rstd", "xn_ready"))
        ln2_stats, ln2_mv, ln2_var, ln2_rstd, x2_ready = (sem(n) for n in ("ln2_stats", "ln2_mv", "ln2_var", "ln2_rstd", "x2_ready"))
        xT_mm, q_mm, k_mm, v_mm, s_mm, pt_mm, av_mm, ot_mm, proj_mm = (
            sem(n) for n in ("xT_mm", "q_mm", "k_mm", "v_mm", "s_mm", "pt_mm", "av_mm", "ot_mm", "proj_mm"))
        xT_ev, q_ev, k_ev, v_ev, pt_ev, exp_done, ot_ev = (
            sem(n) for n in ("xT_ev", "q_ev", "k_ev", "v_ev", "pt_ev", "exp_done", "ot_ev"))
        kbd_ready, rmax_ready, sub_done, rden_ready, av_ev, aux_sum, aux_ready, h1_ready = (
            sem(n) for n in ("kbd_ready", "rmax_ready", "sub_done", "rden_ready", "av_ev", "aux_sum", "aux_ready", "h1_ready"))
        h1_st = [sem(f"h1_st{i}") for i in range(2)]
        x2_st = [sem(f"x2_st{i}") for i in range(2)]
        block = ctx.enter_context(nc.Block())
        CONSTS = 9

        def steps(eng, step):
            for c in range(-2, 3):
                step(0, c)
            with eng.Fori(0, (B - 8) // 4) as k:
                for u in range(4):
                    step(k, 3 + u)
            for c in range(3, 9):
                step((B - 8) // 4, c)

        def is_image(k, c):
            return not isinstance(k, int) or 0 <= 4 * k + c < B

        @block.sync
        def _(sp):
            def load(k, c):
                b, r = 4 * k + c, c % 4
                sp.dma_start(h[r][:, 0, :], h_img[bass.ds(b * n_img, HT), :]).then_inc(h_in[r], 16)
                sp.dma_start(h[r][0:n_img - HT, 1, :], h_img[bass.ds(b * n_img + HT, n_img - HT), :]).then_inc(h_in[r], 16)
                sp.dma_start(h[r][n_img - HT:HT, 1, :], txt[b, :, :]).then_inc(h_in[r], 16)

            def step(k, c):
                s = 4 * k + c
                if is_image(k, c - 1):
                    sp.wait_ge(h1_ready, s)
                    sp.dma_start(h1_out[s - 1, :, :, :], h1[(c - 1) % 2][:, :, :]).then_inc(h1_st[(c - 1) % 2], 16)
                if c + 3 >= 4 and is_image(k, c + 3):
                    load(k, c + 3)
                if is_image(k, c - 1):
                    sp.wait_ge(x2_ready, s)
                    sp.dma_start(x2_out[s - 1, :, :, :], x2[(c - 1) % 2][:, :, :]).then_inc(x2_st[(c - 1) % 2], 16)

            load(0, 0)
            sp.dma_start(wqkv[:, :, :], w_qkv.rearrange("(k p) n -> p k n", p=KC)).then_inc(const_in, 16)
            for b in range(1, 4):
                load(0, b)
            sp.dma_start(wproj[0:KC, :, :], w_proj.rearrange("(k p) n -> p k n", p=KC)).then_inc(const_in, 16)
            sp.dma_start(wproj[KC:KC + 1, 0, :], b_proj.rearrange("(a n) -> a n", a=1)).then_inc(const_in, 16)
            steps(sp, step)
            for i in range(2):
                sp.wait_ge(h1_st[i], 16 * (B // 2))
                sp.wait_ge(x2_st[i], 16 * (B // 2))

        @block.gpsimd
        def _(pool):
            make_identity(nc, ident[:, :], 128, zeroed, consts)
            pool.memset(mhalf[:, :], -0.5).then_inc(consts, 1)
            pool.memset(eps[:, :], EPS).then_inc(consts, 1)
            pool.memset(mask[:, :], 1.0).then_inc(zeroed, 1)
            pool.wait_ge(zeroed, 2)
            pool.affine_select(out=mask[:, :], in_=mask[:, :], compare_op=ALU.is_ge, fill=0.0, base=0,
                               pattern=[[-HD, HC]], channel_multiplier=1).then_inc(zeroed, 1)
            pool.wait_ge(zeroed, 3)
            pool.affine_select(out=mask[:, :], in_=mask[:, :], compare_op=ALU.is_ge, fill=0.0, base=HD - 1,
                               pattern=[[HD, HC]], channel_multiplier=-1).then_inc(consts, 1)
            pool.wait_ge(ones_set, 4)
            for i in range(2):
                v = vbd[i][:, :, :, :, :].rearrange("p t a g v -> p (t a g v)")
                pool.affine_select(out=v, in_=v, compare_op=ALU.not_equal, fill=0.0, base=-(SL - 1),
                                   pattern=[[0, v.shape[1]]], channel_multiplier=1).then_inc(zeroed, 1)
                pool.wait_ge(zeroed, 4 + i)
                last = pool.affine_select(out=v, in_=v, compare_op=ALU.not_equal, fill=0.0, base=-(2 * SL - 1),
                                          pattern=[[0, v.shape[1]]], channel_multiplier=1)
            last.then_inc(consts, 1)

            def rsqrt(b, mv_, var_, rstd_, got, plus, done):
                pool.wait_ge(got, b + 1)
                pool.tensor_tensor(var_[:, :], mv_[:, :, 1], eps[:, :], ALU.add).then_inc(plus, 1)
                pool.wait_ge(plus, b + 1)
                pool.tensor_tensor(rstd_[:, :], var_[:, :], mhalf[:, :], ALU.pow).then_inc(done, 1)

            def step(k, c):
                s = 4 * k + c
                if is_image(k, c + 2):
                    rsqrt(s + 2, mv, vare, rstd, ln_mv, ln_var, ln_rstd)
                if is_image(k, c - 1):
                    rsqrt(s - 1, mv2, vare2, rstd2, ln2_mv, ln2_var, ln2_rstd)
            steps(pool, step)

        @block.tensor
        def _(pe):
            pe.wait_ge(consts, CONSTS)
            pe.wait_ge(const_in, 48)

            def step(k, c):
                s = 4 * k + c
                nxt, cur, prev = is_image(k, c + 1), is_image(k, c), is_image(k, c - 1)
                if nxt:
                    pe.wait_ge(xn_ready, s + 2)
                    wait(pe, v_ev, s + 1)
                    wait(pe, ot_ev, s)
                    for cc in range(2):
                        for t in range(2):
                            last = pe.transpose(x_v[:, cc, t * HT:(t + 1) * HT], xn[:, t, cc * KC:(cc + 1) * KC],
                                                ident[0:HT, 0:HT])
                    last.then_inc(xT_mm, 1)

                def transpose_probs(t):
                    pe.wait_ge(exp_done, 2 * s + 1 + t)
                    wait(pe, av_ev, 2 * s + t)
                    for pr in range(PAIRS):
                        last = pe.transpose(pyz[:, pr, :], prob[t][:, 2 * pr:2 * pr + 2, :].rearrange("p h k -> p (h k)"),
                                            ident[:, :])
                    last.then_inc(pt_mm, 1)

                def weigh_values(t):
                    pe.wait_ge(pt_ev, 2 * s + 1 + t)
                    pe.wait_ge(v_ev, s + 1)
                    for pr in range(PAIRS):
                        last = pe.matmul(pyz[:, pr, 0:2 * VW], pT[t][:, pr, :],
                                         vbd[c % 2][:, t, pr, :, :].rearrange("p g v -> p (g v)"), start=True, stop=True)
                    last.then_inc(av_mm, 1)

                def scores(t):
                    wait(pe, sub_done, 2 * s + 1 + t)
                    for cc in range(2):
                        for gg in range(2):
                            g = 2 * t + gg
                            last = pe.matmul(sc[t][SL * gg:SL * gg + SL, cc, 0:HC * SL],
                                             qT[:, cc, g * SL:(g + 1) * SL],
                                             kbd[:, cc * GROUPS + g, :, :].rearrange("p h k -> p (h k)"),
                                             start=True, stop=True)
                    last.then_inc(s_mm, 1)

                if cur:
                    transpose_probs(0)
                if prev:
                    pe.wait_ge(aux_ready, s)
                    pe.wait_ge(ot_ev, s)
                    pe.wait_ge(k_ev, s)
                    wait(pe, k_ev, s + 1 if cur else 0)
                    for t in range(2):
                        pe.matmul(pr_v[:, t, :], oT[:, 0, t * HT:(t + 1) * HT], wproj[:, 0, :], start=True, stop=False)
                        last = pe.matmul(pr_v[:, t, :], oT[0:KC, 1, t * HT:(t + 1) * HT], wproj[0:KC, 1, :],
                                         start=False, stop=True)
                    last.then_inc(proj_mm, 1)
                if nxt:
                    pe.wait_ge(xT_ev, s + 2)
                    for m in range(2):
                        for cc in range(2):
                            last = pe.matmul(q_v[:, m * 256:(m + 1) * 256], wqkv[:, cc, m * KC:(m + 1) * KC],
                                             xT[:, cc, :, :].rearrange("p g n -> p (g n)"), start=(cc == 0), stop=(cc == 1))
                    last.then_inc(q_mm, 1)
                if cur:
                    weigh_values(0)
                if nxt:
                    wait(pe, h1_ready, s)
                    for m in range(2):
                        for cc in range(2):
                            last = pe.matmul(k_v[:, m * 256:(m + 1) * 256], wqkv[:, cc, CH + m * KC:CH + (m + 1) * KC],
                                             xT[:, cc, :, :].rearrange("p g n -> p (g n)"), start=(cc == 0), stop=(cc == 1))
                    last.then_inc(k_mm, 1)
                    pe.wait_ge(q_ev, s + 2)
                    for t in range(2):
                        for cc in range(2):
                            last = pe.matmul(v_v[:, t, :], xT[:, cc, 2 * t:2 * t + 2, :].rearrange("p g n -> p (g n)"),
                                             wqkv[:, cc, 2 * CH:3 * CH], start=(cc == 0), stop=(cc == 1))
                    last.then_inc(v_mm, 1)
                if cur:
                    transpose_probs(1)
                if nxt:
                    pe.wait_ge(kbd_ready, s + 2)
                    scores(0)
                if cur:
                    weigh_values(1)
                if nxt:
                    scores(1)
                if cur:
                    pe.wait_ge(av_ev, 2 * s + 2)
                    wait(pe, v_ev, s + 2 if nxt else 0)
                    for cc in range(2):
                        for t in range(2):
                            last = pe.transpose(ot_v[:, cc, t * 128:(t + 1) * 128], o[:, t, cc * KC:(cc + 1) * KC], ident[:, :])
                    last.then_inc(ot_mm, 1)
            steps(pe, step)

        @block.scalar
        def _(act):
            act.wait_ge(consts, CONSTS)

            def step(k, c):
                s = 4 * k + c
                nxt, cur = is_image(k, c + 1), is_image(k, c)

                def copy_probs(t):
                    act.wait_ge(pt_mm, 2 * s + 1 + t)
                    wait(act, av_mm, 2 * s - 1 + t)
                    act.activation(pT[t][:, :, :], pyz[:, 0:PAIRS, :], ACT.Copy).then_inc(pt_ev, 1)

                def exponentials(t):
                    act.wait_ge(sub_done, 2 * s + 3 + t)
                    act.activation(prob[t][:, :, 0:KEYS], prob[t][:, :, 0:KEYS], ACT.Exp, scale=float(HD) ** -0.5)\
                       .then_inc(exp_done, 1)

                if nxt:
                    act.wait_ge(xT_mm, s + 2)
                    wait(act, v_mm, s + 1)
                    for cc in range(2):
                        act.activation(xT[:, cc, :, AUX:KEYS], x_v[:, cc, AUX:N].rearrange("p (i g) -> p g i", g=GROUPS), ACT.Copy)
                        a = x_v[:, cc, 0:AUX].rearrange("p (o a) -> p o a", o=1).to_broadcast([KC, GROUPS, AUX])
                        last = act.activation(xT[:, cc, :, 0:AUX], a, ACT.Copy)
                    last.then_inc(xT_ev, 1)
                if cur:
                    copy_probs(0)
                if nxt:
                    act.wait_ge(q_mm, s + 2)
                    wait(act, s_mm, 2 * s + 2)
                    act.activation(qT[:, :, :].rearrange("p c n -> p (c n)"), q_v, ACT.Copy).then_inc(q_ev, 1)
                    act.wait_ge(k_mm, s + 2)
                    wait(act, kbd_ready, s + 1)
                    act.activation(kT[:, :, :].rearrange("p c n -> p (c n)"), k_v, ACT.Copy).then_inc(k_ev, 1)
                    act.wait_ge(v_mm, s + 2)
                    wait(act, av_mm, 2 * s)
                    for gg in range(2):
                        for hh in range(2):
                            src = v_v[64 * gg:64 * gg + 64, :, :].rearrange("p t (a h d) -> p t a h d", h=2, d=HD)[:, :, :, hh, :]
                            dst = vbd[(c + 1) % 2][64 * hh:64 * hh + 64, :, :, gg, hh * HD:(hh + 1) * HD]
                            last = act.activation(dst, src, ACT.Copy)
                    last.then_inc(v_ev, 1)
                if cur:
                    copy_probs(1)
                if nxt:
                    exponentials(0)
                if cur:
                    act.wait_ge(ot_mm, s + 1)
                    wait(act, proj_mm, s)
                    wait(act, aux_ready, s)
                    for cc in range(2):
                        slots = ot_v[:, cc, :].rearrange("p (g n) -> p g n", n=SL)
                        act.activation(oT[0:KC, cc, AUX:N].rearrange("p (i g) -> p g i", g=GROUPS), slots[:, :, AUX:KEYS], ACT.Copy)
                        last = act.activation(auxp[:, cc, :, :], slots[:, :, 0:AUX], ACT.Copy)
                    last.then_inc(ot_ev, 1)
                if nxt:
                    exponentials(1)
            steps(act, step)

        @block.vector
        def _(dve):
            dve.memset(oT[KC:KC + 1, :, :], 1.0).then_inc(consts, 1)
            dve.memset(xT[:, :, :, :], 0.0).then_inc(consts, 1)
            for t in range(2):
                dve.memset(prob[t][:, :, :], 0.0).then_inc(consts, 1)
            for i in range(2):
                last = dve.memset(vbd[i][:, :, :, :, :], 0.0)
            last.then_inc(values_zeroed, 1)
            dve.wait_ge(values_zeroed, 1)
            for i in range(2):
                for hh in range(2):
                    dve.memset(vbd[i][64 * hh:64 * hh + 64, :, :, :, 32 + hh], 1.0).then_inc(ones_set, 1)
            dve.wait_ge(consts, CONSTS)

            def step(k, c):
                s = 4 * k + c
                nxt, cur, prev, two = is_image(k, c + 1), is_image(k, c), is_image(k, c - 1), is_image(k, c + 2)

                def normalise(t):
                    dve.wait_ge(av_mm, 2 * s + 1 + t)
                    for gg in range(2):
                        rows = slice(64 * gg, 64 * gg + 64)
                        last = dve.reciprocal(rden[rows, t, :, :], pyz[rows, 0:PAIRS, gg * VW + 32:gg * VW + 34])
                    last.then_inc(rden_ready, 1)
                    wait(dve, ot_mm, s)
                    dve.wait_ge(rden_ready, 2 * s + 1 + t)
                    for gg in range(2):
                        rows = slice(64 * gg, 64 * gg + 64)
                        last = dve.tensor_tensor(
                            o[rows, t, :].rearrange("p (a h d) -> p a h d", h=2, d=HD),
                            pyz[rows, 0:PAIRS, gg * VW:gg * VW + 32].rearrange("p a (h d) -> p a h d", d=HD),
                            rden[rows, t, :, :].rearrange("p a (h o) -> p a h o", o=1).to_broadcast([64, PAIRS, 2, HD]), ALU.mult)
                    last.then_inc(av_ev, 1)

                def subtract_max(t):
                    dve.wait_ge(s_mm, 2 * s + 3 + t)
                    v = sc[t][:, :, 0:HC * SL].rearrange("p c (h k) -> p c h k", k=SL)[:, :, :, 0:KEYS]
                    dve.tensor_reduce(rmax[:, t, :].rearrange("p (c h) -> p c h", c=2), v, AXX, ALU.max).then_inc(rmax_ready, 1)
                    dve.wait_ge(rmax_ready, 2 * s + 3 + t)
                    wait(dve, pt_mm, 2 * s + 1 + t)
                    dve.tensor_tensor(prob[t][:, :, 0:KEYS].rearrange("p (c h) k -> p c h k", c=2), v,
                                      rmax[:, t, :].rearrange("p (c h o) -> p c h o", c=2, o=1).to_broadcast([128, 2, HC, KEYS]),
                                      ALU.subtract).then_inc(sub_done, 1)

                if prev:
                    dve.wait_ge(ot_ev, s)
                    dve.tensor_reduce(auxs[:, :, :], auxp[:, :, :, :].rearrange("p c g a -> p c a g"), AXX, ALU.add).then_inc(aux_sum, 1)
                    dve.wait_ge(aux_sum, s)
                    dve.tensor_scalar(oT[0:KC, :, 0:AUX], auxs[:, :, :], 1.0 / GROUPS, None, ALU.mult).then_inc(aux_ready, 1)
                    dve.wait_ge(proj_mm, s)
                    wait(dve, h1_st[(c - 1) % 2], 16 * (2 * k + (c - 1) // 2))
                    dve.tensor_tensor(h1[(c - 1) % 2][:, :, :], pr_v, h[(c - 1) % 4][:, :, :], ALU.add).then_inc(h1_ready, 1)
                    dve.wait_ge(h1_ready, s)
                    for t in range(2):
                        last = dve.bn_stats(stats2[:, t, :], h1[(c - 1) % 2][:, t, :])
                    last.then_inc(ln2_stats, 1)
                    wait(dve, ln2_rstd, s - 1)
                    dve.wait_ge(ln2_stats, s)
                    dve.memset(carrier[:, :], 0.0)
                    for t in range(2):
                        last = dve.bn_aggr(mv2[:, t, :], stats2[:, t, :])
                    last.then_inc(ln2_mv, 1)
                if cur:
                    normalise(0)
                if nxt:
                    dve.wait_ge(k_ev, s + 2)
                    wait(dve, s_mm, 2 * s + 2)
                    for hd in range(HC):
                        last = dve.tensor_scalar(kbd[:, :, hd, :], kT[:, :, :], mask[:, hd:hd + 1], None, ALU.mult)
                    last.then_inc(kbd_ready, 1)
                if two:
                    dve.wait_ge(h_in[(c + 2) % 4], 48 * (k + (c + 2) // 4 + 1))
                    for t in range(2):
                        last = dve.bn_stats(stats[:, t, :], h[(c + 2) % 4][:, t, :])
                    last.then_inc(ln_stats, 1)
                    dve.wait_ge(ln_stats, s + 3)
                    dve.memset(carrier[:, :], 0.0)
                    for t in range(2):
                        last = dve.bn_aggr(mv[:, t, :], stats[:, t, :])
                    last.then_inc(ln_mv, 1)
                if prev:
                    dve.wait_ge(ln2_rstd, s)
                    wait(dve, x2_st[(c - 1) % 2], 16 * (2 * k + (c - 1) // 2))
                    for t in range(2):
                        last = dve.tensor_scalar(x2[(c - 1) % 2][:, t, :], h1[(c - 1) % 2][:, t, :], mv2[:, t, 0:1],
                                                 rstd2[:, t:t + 1], ALU.subtract, ALU.mult)
                    last.then_inc(x2_ready, 1)
                if two:
                    dve.wait_ge(ln_rstd, s + 3)
                    wait(dve, xT_mm, s + 2)
                    for t in range(2):
                        last = dve.tensor_scalar(xn[:, t, :], h[(c + 2) % 4][:, t, :], mv[:, t, 0:1],
                                                 rstd[:, t:t + 1], ALU.subtract, ALU.mult)
                    last.then_inc(xn_ready, 1)
                if nxt:
                    subtract_max(0)
                if cur:
                    normalise(1)
                if nxt:
                    subtract_max(1)
            steps(dve, step)


def experts_dense(nc, x2_rows, h1_rows, w_fc, w_pr, w1, w2, router_t, bias, out_rows):
    T, E, J = x2_rows.shape[0], w1.shape[0], 3
    UT = 128 * J
    units = T // UT
    assert units * UT == T
    with ExitStack() as ctx:
        sb = lambda name, shape, dt=F32: ctx.enter_context(nc.sbuf_tensor(name, shape, dt))
        sem = lambda name: ctx.enter_context(nc.semaphore(name))
        pb = lambda name, shape: ctx.enter_context(nc.psum_tensor(name, shape, F32))
        ident = sb("ident_e", [128, 128])
        wup = sb("wup", [KC, E + 1, 2, CH])
        wdn = sb("wdn", [KC, E + 1, 2, CH])
        rt = sb("router_sb", [KC, 2, E])
        bal = sb("balance_sb", [128, E])
        eid = sb("eid", [128, J, E])
        x = sb("x_e", [128, J, CH])
        hres = sb("hres", [128, J, CH])
        xT = sb("xT_e", [KC, 2, UT])
        relu = [sb(f"relu{i}", [KC, 2, UT]) for i in range(2)]
        hT = [sb(f"hT{i}", [KC, 2, UT]) for i in range(2)]
        acc = sb("acc", [128, J, CH])
        sig, sel, oh1, oh2, tmp, comb = (sb(n, [128, J, E]) for n in ("sig", "sel", "oh1", "oh2", "tmp", "comb"))
        m1, i1, wsum = (sb(n, [128, J]) for n in ("m1", "i1", "wsum"))
        hp = [pb(f"hp{i}", [128, 2, 512]) for i in range(2)]
        yp = [pb(f"yp{i}", [128, 4, 256]) for i in range(2)]
        zeroed, consts, w_in = sem("zeroed_e"), sem("consts_e"), sem("w_in_e")
        x_in, res_in, out_st = sem("x_in"), sem("res_in"), sem("out_st")
        x_tr, xT_ev, lg_mm, exp_ev = sem("x_tr"), sem("xT_ev_e"), sem("lg_mm"), sem("exp_ev")
        up_mm, relu_ev, sq_done, dn_mm, acc_done, route = sem("up_mm"), sem("relu_ev"), sem("sq_done"), sem("dn_mm"), sem("acc_done"), sem("route")
        block = ctx.enter_context(nc.Block())
        order = [E] + list(range(E))
        EE = E + 1
        ROUTE = 20

        @block.sync
        def _(sp):
            for dst, src in ((wup[:, E, :, :], w_fc.rearrange("(k p) n -> p k n", p=KC)),
                             (wdn[:, E, :, :], w_pr.rearrange("(k p) n -> p k n", p=KC)),
                             (rt[:, :, :], router_t.rearrange("(k p) e -> p k e", p=KC)),
                             (bal[:, :], bias.rearrange("(o e) -> o e", o=1).to_broadcast([128, E]))):
                sp.dma_start(dst, src).then_inc(w_in, 16)
            for e in range(E):
                sp.dma_start(wup[:, e, :, :], w1[e, :, :].rearrange("(k p) n -> p k n", p=KC)).then_inc(w_in, 16)
                sp.dma_start(wdn[:, e, :, :], w2[e, :, :].rearrange("(k p) n -> p k n", p=KC)).then_inc(w_in, 16)

            def unit(u):
                wait(sp, x_tr, u)
                sp.dma_start(x[:, :, :], x2_rows[bass.ds(u * UT, UT), :].rearrange("(p j) c -> p j c", j=J)).then_inc(x_in, 16)
                wait(sp, acc_done, EE * (u - 1) + 1)
                sp.dma_start(hres[:, :, :], h1_rows[bass.ds(u * UT, UT), :].rearrange("(p j) c -> p j c", j=J)).then_inc(res_in, 16)

            def store(u):
                sp.wait_ge(acc_done, EE * u + EE)
                sp.dma_start(out_rows[bass.ds(u * UT, UT), :].rearrange("(p j) c -> p j c", j=J), acc[:, :, :]).then_inc(out_st, 16)
            unit(0)
            with sp.Fori(1, units) as u:
                unit(u)
                store(u - 1)
            store(units - 1)
            sp.wait_ge(out_st, 16 * units)

        @block.gpsimd
        def _(pool):
            make_identity(nc, ident[:, :], 128, zeroed, consts)
            for e in range(E):
                last = pool.memset(eid[:, :, e], float(e))
            last.then_inc(consts, 1)

            def unit(u):
                for n in range(EE):
                    pool.wait_ge(relu_ev, EE * u + n + 1)
                    wait(pool, dn_mm, EE * u + n - (n > 0))
                    pool.tensor_tensor(hT[n % 2][:, :, :], relu[n % 2][:, :, :], relu[n % 2][:, :, :], ALU.mult)\
                        .then_inc(sq_done, 1)
            unit(0)
            with pool.Fori(1, units) as u:
                unit(u)

        @block.tensor
        def _(pe):
            pe.wait_ge(consts, 2)
            pe.wait_ge(w_in, 16 * (4 + 2 * E))

            def up(u, n):
                g = EE * u + n
                wait(pe, relu_ev, g - (n > 0))
                for m in range(2):
                    for cc in range(2):
                        last = pe.matmul(hp[n % 2][0:KC, m, 0:UT], wup[:, order[n], cc, m * KC:(m + 1) * KC], xT[:, cc, :],
                                         start=(cc == 0), stop=(cc == 1))
                last.then_inc(up_mm, 1)

            def down(u, n):
                g = EE * u + n
                pe.wait_ge(sq_done, g + 1)
                wait(pe, acc_done, g - (n > 0))
                for j in range(J):
                    for cc in range(2):
                        last = pe.matmul(yp[n % 2][:, j, 0:CH], hT[n % 2][:, cc, j * 128:(j + 1) * 128], wdn[:, order[n], cc, :],
                                         start=(cc == 0), stop=(cc == 1))
                last.then_inc(dn_mm, 1)

            def unit(u):
                pe.wait_ge(x_in, 16 * u + 16)
                wait(pe, relu_ev, EE * u)
                for j in range(J):
                    for cc in range(2):
                        last = pe.transpose(hp[1][0:KC, cc, j * 128:(j + 1) * 128], x[:, j, cc * KC:(cc + 1) * KC], ident[:, :])
                last.then_inc(x_tr, 1)
                pe.wait_ge(xT_ev, u + 1)
                for j in range(J):
                    for cc in range(2):
                        last = pe.matmul(hp[1][:, 1, 384 + 8 * j:384 + 8 * j + E], xT[:, cc, j * 128:(j + 1) * 128], rt[:, cc, :],
                                         start=(cc == 0), stop=(cc == 1))
                last.then_inc(lg_mm, 1)
                up(u, 0)
                pe.wait_ge(exp_ev, u + 1)
                for n in range(EE):
                    if n + 1 < EE:
                        up(u, n + 1)
                    down(u, n)
            unit(0)
            with pe.Fori(1, units) as u:
                unit(u)

        @block.scalar
        def _(act):
            def unit(u):
                act.wait_ge(x_tr, u + 1)
                wait(act, up_mm, EE * u)
                act.activation(xT[:, :, :], hp[1][0:KC, :, 0:UT], ACT.Copy).then_inc(xT_ev, 1)
                act.wait_ge(lg_mm, u + 1)
                wait(act, route, ROUTE * u)
                act.activation(sig[:, :, :].rearrange("p j e -> p (j e)"), hp[1][:, 1, 384:384 + J * E], ACT.Exp, scale=-1.0)\
                   .then_inc(exp_ev, 1)
                for n in range(EE):
                    act.wait_ge(up_mm, EE * u + n + 1)
                    wait(act, sq_done, EE * u + n - (n > 0))
                    act.activation(relu[n % 2][:, :, :], hp[n % 2][0:KC, :, 0:UT], ACT.Relu).then_inc(relu_ev, 1)
            unit(0)
            with act.Fori(1, units) as u:
                unit(u)

        @block.vector
        def _(dve):
            dve.wait_ge(consts, 2)
            dve.wait_ge(w_in, 16 * (4 + 2 * E))

            def bc(a):
                return a[:, :].rearrange("p (j o) -> p j o", o=1).to_broadcast([128, J, E])

            def unit(u):
                done = [0]

                def then(instruction):
                    done[0] += 1
                    instruction.then_inc(route, 1)
                    dve.wait_ge(route, ROUTE * u + done[0])
                dve.wait_ge(exp_ev, u + 1)
                wait(dve, acc_done, EE * u)
                then(dve.tensor_scalar(tmp[:, :, :], sig[:, :, :], 1.0, None, ALU.add))
                then(dve.reciprocal(sig[:, :, :], tmp[:, :, :]))
                then(dve.tensor_tensor(sel[:, :, :], sig[:, :, :],
                                       bal[:, :].rearrange("p (o e) -> p o e", o=1).to_broadcast([128, J, E]), ALU.add))
                for oh in (oh1, oh2):
                    then(dve.tensor_reduce(m1[:, :], sel[:, :, :], AXX, ALU.max))
                    then(dve.tensor_tensor(tmp[:, :, :], sel[:, :, :], bc(m1), ALU.is_equal))
                    then(dve.scalar_tensor_tensor(tmp[:, :, :], tmp[:, :, :], -float(E), eid[:, :, :], ALU.mult, ALU.add))
                    then(dve.tensor_reduce(i1[:, :], tmp[:, :, :], AXX, ALU.min))
                    then(dve.tensor_tensor(oh[:, :, :], tmp[:, :, :], bc(i1), ALU.is_equal))
                    if oh is oh1:
                        then(dve.scalar_tensor_tensor(sel[:, :, :], oh[:, :, :], -3e38, sel[:, :, :], ALU.mult, ALU.add))
                then(dve.tensor_tensor(tmp[:, :, :], oh1[:, :, :], oh2[:, :, :], ALU.add))
                then(dve.tensor_tensor(tmp[:, :, :], tmp[:, :, :], sig[:, :, :], ALU.mult))
                then(dve.tensor_reduce(wsum[:, :], tmp[:, :, :], AXX, ALU.add))
                then(dve.tensor_scalar(wsum[:, :], wsum[:, :], 1e-20, None, ALU.add))
                then(dve.reciprocal(wsum[:, :], wsum[:, :]))
                then(dve.tensor_tensor(comb[:, :, :], tmp[:, :, :], bc(wsum), ALU.mult))
                assert done[0] == ROUTE
                for n in range(EE):
                    dve.wait_ge(dn_mm, EE * u + n + 1)
                    if n == 0:
                        dve.wait_ge(res_in, 16 * u + 16)
                        wait(dve, out_st, 16 * u)
                        dve.tensor_tensor(acc[:, :, :], yp[0][:, 0:J, 0:CH], hres[:, :, :], ALU.add).then_inc(acc_done, 1)
                    else:
                        dve.wait_ge(acc_done, EE * u + n)
                        for j in range(J):
                            last = dve.scalar_tensor_tensor(acc[:, j, :], yp[n % 2][:, j, 0:CH], comb[:, j, n - 1:n],
                                                            acc[:, j, :], ALU.mult, ALU.add)
                        last.then_inc(acc_done, 1)
            unit(0)
            with dve.Fori(1, units) as u:
                unit(u)


def program(nc, patches, w_tok, txt, w_qkv, w_proj, b_proj, w_fc, w_pr, w1, w2, router_t, bias, out):
    B, N = out.shape[0], out.shape[1]
    h_img = nc.dram_tensor("h_img_dram", (patches.shape[0] * 128, CH), F32, kind="Internal").ap()
    h1 = nc.dram_tensor("h1_dram", (B * N, CH), F32, kind="Internal").ap()
    x2 = nc.dram_tensor("x2_dram", (B * N, CH), F32, kind="Internal").ap()
    embed_patches(nc, patches, w_tok, h_img)
    images = lambda a: a.rearrange("(b t p) c -> b p t c", t=2, p=N // 2)
    attention(nc, h_img, txt, w_qkv, w_proj, b_proj, images(h1), images(x2))
    experts_dense(nc, x2, h1, w_fc, w_pr, w1, w2, router_t, bias, out.rearrange("b n c -> (b n) c"))


def patch_columns(x):
    starts = np.clip(np.arange(GRID) * PATCH - OVERLAP, 0, IMG - WIN)
    idx = (starts[:, None] + np.arange(WIN)[None, :]).reshape(-1)
    B = x.shape[0]
    g = np.take(np.take(x, idx, axis=1), idx, axis=2).reshape(B, GRID, WIN, GRID, WIN, 3)
    g = g.transpose(0, 1, 3, 2, 4, 5).reshape(B * GRID * GRID // 128, 128, 12, 121)
    return np.ascontiguousarray(g.transpose(0, 3, 2, 1))


def kernel(**inputs):
    import concourse.bacc as bacc
    from concourse.bass_utils import run_bass_kernel_spmd
    a = {n: np.asarray(v) for n, v in inputs.items()}
    B, n_txt = a["txt"].shape[:2]
    N = GRID * GRID + n_txt
    arrays = {
        "patches": patch_columns(a["x"]), "w_tok": a["L0_tok_W"], "txt": a["txt"],
        "w_qkv": a["L0_attn_Wqkv"], "w_proj": a["L0_attn_Wproj"], "b_proj": a["L0_attn_bproj"],
        "w_fc": a["L0_ffn_w_fc_sh"], "w_pr": a["L0_ffn_w_proj_sh"], "w1": a["L0_ffn_w1"], "w2": a["L0_ffn_w2"],
        "router_t": np.ascontiguousarray(a["L0_ffn_router_w"].T), "bias": a["L0_ffn_balance_bias"],
    }
    nc = bacc.Bacc("TRN2", target_bir_lowering=False, num_devices=1)
    args = [nc.dram_tensor(n, v.shape, mybir.dt.from_np(v.dtype), kind="ExternalInput").ap() for n, v in arrays.items()]
    out = nc.dram_tensor("out_dram", (B, N, CH), F32, kind="ExternalOutput").ap()
    program(nc, *args, out)
    return run_bass_kernel_spmd(nc, [arrays], core_ids=[0]).results[0]["out_dram"]
```

```python
import numpy as np
import concourse.bass as bass
from concourse import mybir
from concourse.alu_op_type import AluOpType as ALU
from contextlib import ExitStack

F32 = mybir.dt.float32
ACT = mybir.ActivationFunctionType
AXX = mybir.AxisListType.X

GRID, IMG, WIN, PATCH, OVERLAP = 14, 224, 22, 16, 3
CH = 192
KC = 96
HEADS, HD = 12, 16
AUX, GROUPS = 8, 4
EPS = 1e-5
SLOTS = 256


def wait(eng, sem, value):
    if isinstance(value, int) and value <= 0:
        return
    eng.wait_ge(sem, value)


def make_identity(nc, ident, n, zeroed, ready):
    nc.gpsimd.memset(ident, 0.0).then_inc(zeroed, 1)
    nc.gpsimd.wait_ge(zeroed, 1)
    nc.gpsimd.affine_select(out=ident, in_=ident, compare_op=ALU.not_equal, fill=1.0, base=0,
                            pattern=[[-1, n]], channel_multiplier=1).then_inc(ready, 1)


def embed_patches(nc, patches, w_tok, h_img):
    chunks, kp, kt, m = patches.shape
    RING = 7
    rounds = chunks // RING
    assert chunks == rounds * RING and m == 128
    with ExitStack() as ctx:
        sb = lambda name, shape: ctx.enter_context(nc.sbuf_tensor(name, shape, F32))
        sem = lambda name: ctx.enter_context(nc.semaphore(name))
        w = sb("w_tok_sb", [kp, kt, CH])
        pat = [sb(f"pat{i}", [kp, kt, m]) for i in range(RING)]
        emb = [sb(f"emb{i}", [m, CH]) for i in range(RING)]
        ps = [ctx.enter_context(nc.psum_tensor(f"emb_ps{i}", [m, CH], F32)) for i in range(RING)]
        w_in = sem("w_tok_in")
        pat_in = [sem(f"pat_in{i}") for i in range(RING)]
        emb_out = [sem(f"emb_out{i}") for i in range(RING)]
        emb_mm, emb_ev = sem("emb_mm"), sem("emb_ev")
        block = ctx.enter_context(nc.Block())

        @block.sync
        def _(sp):
            def load(k, i):
                sp.dma_start(pat[i][:, :, :], patches[k * RING + i, :, :, :]).then_inc(pat_in[i], 16)
            sp.dma_start(w[:, :, :], w_tok.rearrange("(t p) c -> p t c", p=kp)).then_inc(w_in, 16)
            for i in range(RING):
                load(0, i)
            with sp.Fori(1, rounds) as k:
                for i in range(RING):
                    sp.wait_ge(emb_mm, (k - 1) * RING + i + 1)
                    load(k, i)

        @block.tensor
        def _(pe):
            def tile(k, i):
                pe.wait_ge(pat_in[i], 16 * k + 16)
                wait(pe, emb_ev, k * RING + i + 1 - RING)
                for t in range(kt):
                    last = pe.matmul(ps[i][:, :], pat[i][:, t, :], w[:, t, :], start=(t == 0), stop=(t == kt - 1))
                last.then_inc(emb_mm, 1)
            pe.wait_ge(w_in, 16)
            for i in range(RING):
                tile(0, i)
            with pe.Fori(1, rounds) as k:
                for i in range(RING):
                    tile(k, i)

        @block.vector
        def _(dve):
            def tile(k, i):
                dve.wait_ge(emb_mm, k * RING + i + 1)
                wait(dve, emb_out[i], 16 * k)
                dve.tensor_copy(emb[i][:, :], ps[i][:, :]).then_inc(emb_ev, 1)
            for i in range(RING):
                tile(0, i)
            with dve.Fori(1, rounds) as k:
                for i in range(RING):
                    tile(k, i)

        @block.scalar
        def _(act):
            def store(k, i):
                act.wait_ge(emb_ev, k * RING + i + 1)
                act.dma_start(h_img[bass.ds((k * RING + i) * m, m), :], emb[i][:, :]).then_inc(emb_out[i], 16)
            with act.Fori(0, rounds) as k:
                for i in range(RING):
                    store(k, i)
            for i in range(RING):
                act.wait_ge(emb_out[i], 16 * rounds)


def attention(nc, h_img, txt, w_qkv, w_proj, b_proj, h1_out, x2_out):
    B, n_txt = txt.shape[0], txt.shape[1]
    n_img = h_img.shape[0] // B
    N = n_img + n_txt
    HT = N // 2
    INNER = (N - AUX) // GROUPS
    KEYS = AUX + INNER
    SL = 64
    HC = KC // HD
    PAIRS = HEADS // 2
    VW = 48
    assert B % 4 == 0 and 2 * HT == N and KEYS == SL - 1
    with ExitStack() as ctx:
        sb = lambda name, shape: ctx.enter_context(nc.sbuf_tensor(name, shape, F32))
        sem = lambda name: ctx.enter_context(nc.semaphore(name))
        pb = lambda name, shape: ctx.enter_context(nc.psum_tensor(name, shape, F32))
        ident = sb("ident_a", [128, 128])
        wqkv = sb("wqkv_sb", [KC, 2, 3 * CH])
        wproj = sb("wproj_sb", [KC + 1, 2, CH])
        mask = sb("head_mask", [KC, HC])
        h = [sb(f"h_sb{i}", [HT, 2, CH]) for i in range(4)]
        stats, mv = sb("stats", [HT, 2, 6]), sb("mv", [HT, 2, 2])
        vare, rstd = sb("vare", [HT, 2]), sb("rstd", [HT, 2])
        stats2, mv2 = sb("stats2", [HT, 2, 6]), sb("mv2", [HT, 2, 2])
        vare2, rstd2 = sb("vare2", [HT, 2]), sb("rstd2", [HT, 2])
        mhalf, eps = sb("minus_half", [HT, 2]), sb("eps", [HT, 2])
        carrier = sb("carrier", [HT, 1])
        xn = sb("xn", [HT, 2, CH])
        xT = sb("xT", [KC, 2, GROUPS, SL])
        qT = sb("qT", [KC, 2, GROUPS * SL])
        kT = sb("kT", [KC, 2 * GROUPS, SL])
        kbd = sb("kbd", [KC, 2 * GROUPS, HC, SL])
        vbd = [sb(f"vbd{i}", [128, 2, PAIRS, 2, VW]) for i in range(2)]
        prob = [sb(f"prob{t}", [128, HEADS, SL]) for t in range(2)]
        rmax = sb("rowmax", [128, 2, HEADS])
        pT = [sb(f"pT{t}", [128, PAIRS, 128]) for t in range(2)]
        rden = sb("rden", [128, 2, PAIRS, 2])
        o = sb("o", [128, 2, CH])
        oT = sb("oT", [KC + 1, 2, N])
        auxp = sb("auxp", [KC, 2, GROUPS, AUX])
        auxs = sb("auxs", [KC, 2, AUX])
        h1 = [sb(f"h1_{i}", [HT, 2, CH]) for i in range(2)]
        x2 = [sb(f"x2_{i}", [HT, 2, CH]) for i in range(2)]
        sc = [pb(f"sc{t}", [128, 2, 512]) for t in range(2)]
        px = pb("px", [128, 512])
        pw = pb("pw", [128, 512])
        pyz = pb("pyz", [128, 8, 128])
        x_v = px[0:KC, 0:2 * N].rearrange("p (c n) -> p c n", c=2)
        k_v = px[0:KC, :]
        v_v = px[:, 0:2 * CH].rearrange("p (t c) -> p t c", t=2)
        ot_v = pw[0:KC, :].rearrange("p (c n) -> p c n", c=2)
        q_v = pw[0:KC, :]
        pr_v = pw[0:HT, 0:2 * CH].rearrange("p (t c) -> p t c", t=2)

        zeroed, consts, const_in = sem("zeroed_a"), sem("consts_a"), sem("const_in")
        values_zeroed, ones_set = sem("values_zeroed"), sem("ones_set")
        h_in = [sem(f"h_in{i}") for i in range(4)]
        ln_stats, ln_mv, ln_var, ln_rstd, xn_ready = (sem(n) for n in ("ln_stats", "ln_mv", "ln_var", "ln_rstd", "xn_ready"))
        ln2_stats, ln2_mv, ln2_var, ln2_rstd, x2_ready = (sem(n) for n in ("ln2_stats", "ln2_mv", "ln2_var", "ln2_rstd", "x2_ready"))
        xT_mm, q_mm, k_mm, v_mm, s_mm, pt_mm, av_mm, ot_mm, proj_mm = (
            sem(n) for n in ("xT_mm", "q_mm", "k_mm", "v_mm", "s_mm", "pt_mm", "av_mm", "ot_mm", "proj_mm"))
        xT_ev, q_ev, k_ev, v_ev, pt_ev, exp_done, ot_ev = (
            sem(n) for n in ("xT_ev", "q_ev", "k_ev", "v_ev", "pt_ev", "exp_done", "ot_ev"))
        kbd_ready, rmax_ready, sub_done, rden_ready, av_ev, aux_sum, aux_ready, h1_ready = (
            sem(n) for n in ("kbd_ready", "rmax_ready", "sub_done", "rden_ready", "av_ev", "aux_sum", "aux_ready", "h1_ready"))
        h1_st = [sem(f"h1_st{i}") for i in range(2)]
        x2_st = [sem(f"x2_st{i}") for i in range(2)]
        block = ctx.enter_context(nc.Block())
        CONSTS = 9

        def steps(eng, step):
            for c in range(-2, 3):
                step(0, c)
            with eng.Fori(0, (B - 8) // 4) as k:
                for u in range(4):
                    step(k, 3 + u)
            for c in range(3, 9):
                step((B - 8) // 4, c)

        def is_image(k, c):
            return not isinstance(k, int) or 0 <= 4 * k + c < B

        @block.sync
        def _(sp):
            def load(k, c):
                b, r = 4 * k + c, c % 4
                sp.dma_start(h[r][:, 0, :], h_img[bass.ds(b * n_img, HT), :]).then_inc(h_in[r], 16)
                sp.dma_start(h[r][0:n_img - HT, 1, :], h_img[bass.ds(b * n_img + HT, n_img - HT), :]).then_inc(h_in[r], 16)
                sp.dma_start(h[r][n_img - HT:HT, 1, :], txt[b, :, :]).then_inc(h_in[r], 16)

            def step(k, c):
                s = 4 * k + c
                if is_image(k, c - 1):
                    sp.wait_ge(h1_ready, s)
                    sp.dma_start(h1_out[s - 1, :, :, :], h1[(c - 1) % 2][:, :, :]).then_inc(h1_st[(c - 1) % 2], 16)
                if c + 3 >= 4 and is_image(k, c + 3):
                    load(k, c + 3)
                if is_image(k, c - 1):
                    sp.wait_ge(x2_ready, s)
                    sp.dma_start(x2_out[s - 1, :, :, :], x2[(c - 1) % 2][:, :, :]).then_inc(x2_st[(c - 1) % 2], 16)

            load(0, 0)
            sp.dma_start(wqkv[:, :, :], w_qkv.rearrange("(k p) n -> p k n", p=KC)).then_inc(const_in, 16)
            for b in range(1, 4):
                load(0, b)
            sp.dma_start(wproj[0:KC, :, :], w_proj.rearrange("(k p) n -> p k n", p=KC)).then_inc(const_in, 16)
            sp.dma_start(wproj[KC:KC + 1, 0, :], b_proj.rearrange("(a n) -> a n", a=1)).then_inc(const_in, 16)
            steps(sp, step)
            for i in range(2):
                sp.wait_ge(h1_st[i], 16 * (B // 2))
                sp.wait_ge(x2_st[i], 16 * (B // 2))

        @block.gpsimd
        def _(pool):
            make_identity(nc, ident[:, :], 128, zeroed, consts)
            pool.memset(mhalf[:, :], -0.5).then_inc(consts, 1)
            pool.memset(eps[:, :], EPS).then_inc(consts, 1)
            pool.memset(mask[:, :], 1.0).then_inc(zeroed, 1)
            pool.wait_ge(zeroed, 2)
            pool.affine_select(out=mask[:, :], in_=mask[:, :], compare_op=ALU.is_ge, fill=0.0, base=0,
                               pattern=[[-HD, HC]], channel_multiplier=1).then_inc(zeroed, 1)
            pool.wait_ge(zeroed, 3)
            pool.affine_select(out=mask[:, :], in_=mask[:, :], compare_op=ALU.is_ge, fill=0.0, base=HD - 1,
                               pattern=[[HD, HC]], channel_multiplier=-1).then_inc(consts, 1)
            pool.wait_ge(ones_set, 4)
            for i in range(2):
                v = vbd[i][:, :, :, :, :].rearrange("p t a g v -> p (t a g v)")
                pool.affine_select(out=v, in_=v, compare_op=ALU.not_equal, fill=0.0, base=-(SL - 1),
                                   pattern=[[0, v.shape[1]]], channel_multiplier=1).then_inc(zeroed, 1)
                pool.wait_ge(zeroed, 4 + i)
                last = pool.affine_select(out=v, in_=v, compare_op=ALU.not_equal, fill=0.0, base=-(2 * SL - 1),
                                          pattern=[[0, v.shape[1]]], channel_multiplier=1)
            last.then_inc(consts, 1)

            def rsqrt(b, mv_, var_, rstd_, got, plus, done):
                pool.wait_ge(got, b + 1)
                pool.tensor_tensor(var_[:, :], mv_[:, :, 1], eps[:, :], ALU.add).then_inc(plus, 1)
                pool.wait_ge(plus, b + 1)
                pool.tensor_tensor(rstd_[:, :], var_[:, :], mhalf[:, :], ALU.pow).then_inc(done, 1)

            def step(k, c):
                s = 4 * k + c
                if is_image(k, c + 2):
                    rsqrt(s + 2, mv, vare, rstd, ln_mv, ln_var, ln_rstd)
                if is_image(k, c - 1):
                    rsqrt(s - 1, mv2, vare2, rstd2, ln2_mv, ln2_var, ln2_rstd)
            steps(pool, step)

        @block.tensor
        def _(pe):
            pe.wait_ge(consts, CONSTS)
            pe.wait_ge(const_in, 48)

            def step(k, c):
                s = 4 * k + c
                two, nxt, cur, prev = (is_image(k, c + i) for i in (2, 1, 0, -1))

                def transpose_probs(t):
                    pe.wait_ge(exp_done, 2 * s + 1 + t)
                    wait(pe, av_ev, 2 * s + t)
                    for pr in range(PAIRS):
                        last = pe.transpose(pyz[:, pr, :], prob[t][:, 2 * pr:2 * pr + 2, :].rearrange("p h k -> p (h k)"),
                                            ident[:, :])
                    last.then_inc(pt_mm, 1)

                def weigh_values(t):
                    pe.wait_ge(pt_ev, 2 * s + 1 + t)
                    pe.wait_ge(v_ev, s + 1)
                    for pr in range(PAIRS):
                        last = pe.matmul(pyz[:, pr, 0:2 * VW], pT[t][:, pr, :],
                                         vbd[c % 2][:, t, pr, :, :].rearrange("p g v -> p (g v)"), start=True, stop=True)
                    last.then_inc(av_mm, 1)

                def scores(t):
                    wait(pe, sub_done, 2 * s + 1 + t)
                    for cc in range(2):
                        for gg in range(2):
                            g = 2 * t + gg
                            last = pe.matmul(sc[t][SL * gg:SL * gg + SL, cc, 0:HC * SL],
                                             qT[:, cc, g * SL:(g + 1) * SL],
                                             kbd[:, cc * GROUPS + g, :, :].rearrange("p h k -> p (h k)"),
                                             start=True, stop=True)
                    last.then_inc(s_mm, 1)

                if nxt:
                    pe.wait_ge(xT_ev, s + 2)
                    for m in range(2):
                        for cc in range(2):
                            last = pe.matmul(k_v[:, m * 256:(m + 1) * 256], wqkv[:, cc, CH + m * KC:CH + (m + 1) * KC],
                                             xT[:, cc, :, :].rearrange("p g n -> p (g n)"), start=(cc == 0), stop=(cc == 1))
                    last.then_inc(k_mm, 1)
                if cur:
                    transpose_probs(0)
                if prev:
                    pe.wait_ge(aux_ready, s)
                    pe.wait_ge(ot_ev, s)
                    for t in range(2):
                        pe.matmul(pr_v[:, t, :], oT[:, 0, t * HT:(t + 1) * HT], wproj[:, 0, :], start=True, stop=False)
                        last = pe.matmul(pr_v[:, t, :], oT[0:KC, 1, t * HT:(t + 1) * HT], wproj[0:KC, 1, :],
                                         start=False, stop=True)
                    last.then_inc(proj_mm, 1)
                if cur:
                    weigh_values(0)
                if nxt:
                    wait(pe, h1_ready, s)
                    wait(pe, ot_ev, s)
                    for m in range(2):
                        for cc in range(2):
                            last = pe.matmul(q_v[:, m * 256:(m + 1) * 256], wqkv[:, cc, m * KC:(m + 1) * KC],
                                             xT[:, cc, :, :].rearrange("p g n -> p (g n)"), start=(cc == 0), stop=(cc == 1))
                    last.then_inc(q_mm, 1)
                    pe.wait_ge(k_ev, s + 2)
                    for t in range(2):
                        for cc in range(2):
                            last = pe.matmul(v_v[:, t, :], xT[:, cc, 2 * t:2 * t + 2, :].rearrange("p g n -> p (g n)"),
                                             wqkv[:, cc, 2 * CH:3 * CH], start=(cc == 0), stop=(cc == 1))
                    last.then_inc(v_mm, 1)
                if cur:
                    transpose_probs(1)
                if nxt:
                    pe.wait_ge(kbd_ready, s + 2)
                    pe.wait_ge(q_ev, s + 2)
                    scores(0)
                if cur:
                    weigh_values(1)
                if two:
                    pe.wait_ge(xn_ready, s + 3)
                    wait(pe, v_ev, s + 2)
                    for cc in range(2):
                        for t in range(2):
                            last = pe.transpose(x_v[:, cc, t * HT:(t + 1) * HT], xn[:, t, cc * KC:(cc + 1) * KC],
                                                ident[0:HT, 0:HT])
                    last.then_inc(xT_mm, 1)
                if nxt:
                    scores(1)
                if cur:
                    pe.wait_ge(av_ev, 2 * s + 2)
                    pe.wait_ge(q_ev, s + 1)
                    for cc in range(2):
                        for t in range(2):
                            last = pe.transpose(ot_v[:, cc, t * 128:(t + 1) * 128], o[:, t, cc * KC:(cc + 1) * KC], ident[:, :])
                    last.then_inc(ot_mm, 1)
            steps(pe, step)

        @block.scalar
        def _(act):
            act.wait_ge(consts, CONSTS)

            def step(k, c):
                s = 4 * k + c
                two, nxt, cur = (is_image(k, c + i) for i in (2, 1, 0))

                def copy_probs(t):
                    act.wait_ge(pt_mm, 2 * s + 1 + t)
                    wait(act, av_mm, 2 * s - 1 + t)
                    act.activation(pT[t][:, :, :], pyz[:, 0:PAIRS, :], ACT.Copy).then_inc(pt_ev, 1)

                def exponentials(i, t):
                    act.wait_ge(sub_done, 2 * i + 1 + t)
                    act.activation(prob[t][:, :, 0:KEYS], prob[t][:, :, 0:KEYS], ACT.Exp, scale=float(HD) ** -0.5)\
                       .then_inc(exp_done, 1)

                if nxt:
                    act.wait_ge(k_mm, s + 2)
                    wait(act, kbd_ready, s + 1)
                    act.activation(kT[:, :, :].rearrange("p c n -> p (c n)"), k_v, ACT.Copy).then_inc(k_ev, 1)
                if cur:
                    exponentials(s, 1)
                    copy_probs(0)
                if nxt:
                    act.wait_ge(q_mm, s + 2)
                    wait(act, s_mm, 2 * s + 2)
                    act.activation(qT[:, :, :].rearrange("p c n -> p (c n)"), q_v, ACT.Copy).then_inc(q_ev, 1)
                    act.wait_ge(v_mm, s + 2)
                    wait(act, av_mm, 2 * s)
                    for gg in range(2):
                        for hh in range(2):
                            src = v_v[64 * gg:64 * gg + 64, :, :].rearrange("p t (a h d) -> p t a h d", h=2, d=HD)[:, :, :, hh, :]
                            dst = vbd[(c + 1) % 2][64 * hh:64 * hh + 64, :, :, gg, hh * HD:(hh + 1) * HD]
                            last = act.activation(dst, src, ACT.Copy)
                    last.then_inc(v_ev, 1)
                if cur:
                    copy_probs(1)
                if two:
                    act.wait_ge(xT_mm, s + 3)
                    wait(act, v_mm, s + 2)
                    for cc in range(2):
                        act.activation(xT[:, cc, :, AUX:KEYS], x_v[:, cc, AUX:N].rearrange("p (i g) -> p g i", g=GROUPS), ACT.Copy)
                        a = x_v[:, cc, 0:AUX].rearrange("p (o a) -> p o a", o=1).to_broadcast([KC, GROUPS, AUX])
                        last = act.activation(xT[:, cc, :, 0:AUX], a, ACT.Copy)
                    last.then_inc(xT_ev, 1)
                if nxt:
                    exponentials(s + 1, 0)
                if cur:
                    act.wait_ge(ot_mm, s + 1)
                    wait(act, proj_mm, s)
                    wait(act, aux_ready, s)
                    for cc in range(2):
                        slots = ot_v[:, cc, :].rearrange("p (g n) -> p g n", n=SL)
                        act.activation(oT[0:KC, cc, AUX:N].rearrange("p (i g) -> p g i", g=GROUPS), slots[:, :, AUX:KEYS], ACT.Copy)
                        last = act.activation(auxp[:, cc, :, :], slots[:, :, 0:AUX], ACT.Copy)
                    last.then_inc(ot_ev, 1)
            steps(act, step)

        @block.vector
        def _(dve):
            dve.memset(oT[KC:KC + 1, :, :], 1.0).then_inc(consts, 1)
            dve.memset(xT[:, :, :, :], 0.0).then_inc(consts, 1)
            for t in range(2):
                dve.memset(prob[t][:, :, :], 0.0).then_inc(consts, 1)
            for i in range(2):
                last = dve.memset(vbd[i][:, :, :, :, :], 0.0)
            last.then_inc(values_zeroed, 1)
            dve.wait_ge(values_zeroed, 1)
            for i in range(2):
                for hh in range(2):
                    dve.memset(vbd[i][64 * hh:64 * hh + 64, :, :, :, 32 + hh], 1.0).then_inc(ones_set, 1)
            dve.wait_ge(consts, CONSTS)

            def step(k, c):
                s = 4 * k + c
                nxt, cur, prev, two = is_image(k, c + 1), is_image(k, c), is_image(k, c - 1), is_image(k, c + 2)

                def normalise(t):
                    dve.wait_ge(av_mm, 2 * s + 1 + t)
                    for gg in range(2):
                        rows = slice(64 * gg, 64 * gg + 64)
                        last = dve.reciprocal(rden[rows, t, :, :], pyz[rows, 0:PAIRS, gg * VW + 32:gg * VW + 34])
                    last.then_inc(rden_ready, 1)
                    wait(dve, ot_mm, s)
                    dve.wait_ge(rden_ready, 2 * s + 1 + t)
                    for gg in range(2):
                        rows = slice(64 * gg, 64 * gg + 64)
                        last = dve.tensor_tensor(
                            o[rows, t, :].rearrange("p (a h d) -> p a h d", h=2, d=HD),
                            pyz[rows, 0:PAIRS, gg * VW:gg * VW + 32].rearrange("p a (h d) -> p a h d", d=HD),
                            rden[rows, t, :, :].rearrange("p a (h o) -> p a h o", o=1).to_broadcast([64, PAIRS, 2, HD]), ALU.mult)
                    last.then_inc(av_ev, 1)

                def subtract_max(t):
                    dve.wait_ge(s_mm, 2 * s + 3 + t)
                    v = sc[t][:, :, 0:HC * SL].rearrange("p c (h k) -> p c h k", k=SL)[:, :, :, 0:KEYS]
                    dve.tensor_reduce(rmax[:, t, :].rearrange("p (c h) -> p c h", c=2), v, AXX, ALU.max).then_inc(rmax_ready, 1)
                    dve.wait_ge(rmax_ready, 2 * s + 3 + t)
                    wait(dve, pt_mm, 2 * s + 1 + t)
                    dve.tensor_tensor(prob[t][:, :, 0:KEYS].rearrange("p (c h) k -> p c h k", c=2), v,
                                      rmax[:, t, :].rearrange("p (c h o) -> p c h o", c=2, o=1).to_broadcast([128, 2, HC, KEYS]),
                                      ALU.subtract).then_inc(sub_done, 1)

                if two:
                    dve.wait_ge(h_in[(c + 2) % 4], 48 * (k + (c + 2) // 4 + 1))
                    for t in range(2):
                        last = dve.bn_stats(stats[:, t, :], h[(c + 2) % 4][:, t, :])
                    last.then_inc(ln_stats, 1)
                    dve.wait_ge(ln_stats, s + 3)
                    dve.memset(carrier[:, :], 0.0)
                    for t in range(2):
                        last = dve.bn_aggr(mv[:, t, :], stats[:, t, :])
                    last.then_inc(ln_mv, 1)
                if prev:
                    dve.wait_ge(proj_mm, s)
                    wait(dve, h1_st[(c - 1) % 2], 16 * (2 * k + (c - 1) // 2))
                    dve.tensor_tensor(h1[(c - 1) % 2][:, :, :], pr_v, h[(c - 1) % 4][:, :, :], ALU.add).then_inc(h1_ready, 1)
                if nxt:
                    dve.wait_ge(k_ev, s + 2)
                    wait(dve, s_mm, 2 * s + 2)
                    for hd in range(HC):
                        last = dve.tensor_scalar(kbd[:, :, hd, :], kT[:, :, :], mask[:, hd:hd + 1], None, ALU.mult)
                    last.then_inc(kbd_ready, 1)
                if cur:
                    normalise(0)
                if two:
                    dve.wait_ge(ln_rstd, s + 3)
                    wait(dve, xT_mm, s + 2)
                    for t in range(2):
                        last = dve.tensor_scalar(xn[:, t, :], h[(c + 2) % 4][:, t, :], mv[:, t, 0:1],
                                                 rstd[:, t:t + 1], ALU.subtract, ALU.mult)
                    last.then_inc(xn_ready, 1)
                if prev:
                    dve.wait_ge(h1_ready, s)
                    for t in range(2):
                        last = dve.bn_stats(stats2[:, t, :], h1[(c - 1) % 2][:, t, :])
                    last.then_inc(ln2_stats, 1)
                    wait(dve, ln2_rstd, s - 1)
                    dve.wait_ge(ln2_stats, s)
                    dve.memset(carrier[:, :], 0.0)
                    for t in range(2):
                        last = dve.bn_aggr(mv2[:, t, :], stats2[:, t, :])
                    last.then_inc(ln2_mv, 1)
                if cur:
                    normalise(1)
                if nxt:
                    subtract_max(0)
                    subtract_max(1)
                if cur:
                    dve.wait_ge(ot_ev, s + 1)
                    dve.tensor_reduce(auxs[:, :, :], auxp[:, :, :, :].rearrange("p c g a -> p c a g"), AXX, ALU.add).then_inc(aux_sum, 1)
                    dve.wait_ge(aux_sum, s + 1)
                    dve.tensor_scalar(oT[0:KC, :, 0:AUX], auxs[:, :, :], 1.0 / GROUPS, None, ALU.mult).then_inc(aux_ready, 1)
                if prev:
                    dve.wait_ge(ln2_rstd, s)
                    wait(dve, x2_st[(c - 1) % 2], 16 * (2 * k + (c - 1) // 2))
                    for t in range(2):
                        last = dve.tensor_scalar(x2[(c - 1) % 2][:, t, :], h1[(c - 1) % 2][:, t, :], mv2[:, t, 0:1],
                                                 rstd2[:, t:t + 1], ALU.subtract, ALU.mult)
                    last.then_inc(x2_ready, 1)
            steps(dve, step)


def region_rows(T):
    return T + SLOTS


def shared_expert_and_routing(nc, x2_rows, h1_rows, w_fc, w_pr, router_t, bias, hs_rows, slots, pos_out, weight_out, tiles_out, steps_out):
    T, E, J = x2_rows.shape[0], router_t.shape[1], 3
    UT = 128 * J
    units = T // UT
    REGION = region_rows(T)
    NT = tiles_out.shape[1]
    MOST = -(-T // SLOTS)
    assert units * UT == T and units >= 8
    I32, BF16 = mybir.dt.int32, mybir.dt.bfloat16
    with ExitStack() as ctx:
        sb = lambda name, shape, dt=F32: ctx.enter_context(nc.sbuf_tensor(name, shape, dt))
        sem = lambda name: ctx.enter_context(nc.semaphore(name))
        pb = lambda name, shape: ctx.enter_context(nc.psum_tensor(name, shape, F32))
        ident = sb("ident_r", [128, 128])
        before = sb("before", [128, 128], BF16)
        ones = sb("ones_r", [128, 128], BF16)
        wup, wdn = sb("wup_s", [KC, 2, CH]), sb("wdn_s", [KC, 2, CH])
        rt = sb("router_sb", [KC, 2, E])
        bal = sb("balance_sb", [128, E])
        eid = sb("eid", [128, J, E])
        carrier = sb("carrier_r", [128, 1])
        x = [sb(f"x_r{i}", [128, J, CH]) for i in range(4)]
        hres = [sb(f"hres{i}", [128, J, CH]) for i in range(2)]
        hs = [sb(f"hs{i}", [128, J, CH]) for i in range(2)]
        xT = sb("xT_r", [KC, 2, UT])
        relu, hT = sb("relu_r", [KC, 2, UT]), sb("hT_r", [KC, 2, UT])
        expo, sig, sel, both = (sb(n, [128, J, E]) for n in ("expo", "sig", "sel", "both"))
        top = sb("top", [128, J, 8])
        topi = sb("topi", [128, J, 8], mybir.dt.uint32)
        pick = [sb(f"pick{i}", [128, 2, J, E]) for i in range(2)]
        mask = [sb(f"mask{i}", [128, J, E], BF16) for i in range(2)]
        prod, prod2 = sb("prod", [128, 2, J, E]), sb("prod2", [128, 2, J, E])
        chosen = sb("chosen", [128, 2, J])
        wsum = sb("wsum", [128, J])
        weight = [sb(f"weight{i}", [128, 2, J]) for i in range(2)]
        start = [sb(f"start{i}", [128, J, E]) for i in range(2)]
        rows = sb("rows", [128, J, E])
        posf = [sb(f"posf{i}", [128, 2, J]) for i in range(2)]
        posi = [sb(f"posi{i}", [128, 2, J], I32) for i in range(2)]
        zrow = sb("zrow", [128, CH])
        count = sb("count", [128, E])
        grid, over = sb("grid", [128, E, MOST]), sb("over", [128, E, MOST])
        ntile, ends, step_e, zeros_e = (sb(n, [128, E]) for n in ("ntile", "ends", "step_e", "zeros_e"))
        tnum = sb("tnum", [128, NT, E])
        past, skip = sb("past", [128, NT, E]), sb("skip", [128, NT, E])
        tbase, texp = sb("tbase", [128, NT]), sb("texp", [128, NT])
        tile_i = sb("tile_i", [128, 2, NT], I32)
        lane = sb("lane", [128, 2], F32)
        units_begun = sem("units_begun")
        padf = sb("padf", [128, 2, E])
        padi = sb("padi", [128, 2 * E], I32)
        tp = pb("tp", [128, 2, 512])
        hp = pb("hp", [128, 2, 512])
        yp = pb("yp", [128, 4, 256])
        lp = pb("lp", [128, 512])
        rp = pb("rp", [128, 512])
        logits = lp[:, 0:J * E]
        rank = rp[:, 0:J * E].rearrange("p (j e) -> p j e", j=J)
        total = rp[:, J * E:2 * J * E].rearrange("p (j e) -> p j e", j=J)

        zeroed, consts, dconsts, w_in = sem("zeroed_r"), sem("consts_r"), sem("dconsts_r"), sem("w_in_r")
        x_in = [sem(f"x_in{i}") for i in range(4)]
        sent = [sem(f"sent{i}") for i in range(4)]
        res_in = [sem(f"res_in{i}") for i in range(2)]
        hs_st = [sem(f"hs_st{i}") for i in range(2)]
        meta_st = [sem(f"meta_st{i}") for i in range(2)]
        x_tr, xT_ev, up_mm, relu_ev, sq_done, lg_mm, exp_ev, rk_mm, dn_mm = (
            sem(n) for n in ("x_tr", "xT_ev_r", "up_mm", "relu_ev", "sq_done", "lg_mm", "exp_ev", "rk_mm", "dn_mm"))
        route, mask_ready, weight_ready, place, summed, pos_ready, hs_ready = (
            sem(n) for n in ("route", "mask_ready", "weight_ready", "place", "summed", "pos_ready", "hs_ready"))
        plan, pad_ready, pad_sent, tiles_ready, tail_st, tiles_st = (
            sem(n) for n in ("plan", "pad_ready", "pad_sent", "tiles_ready", "tail_st", "tiles_st"))
        block = ctx.enter_context(nc.Block())
        ROUTE, PLACE = 11, 5
        CONSTS, DCONSTS, LOADS = 7, 4, 64

        def steps(eng, step):
            whole = (units - 3) // 4
            for c in (-1, 0):
                step(0, c)
            with eng.Fori(0, whole) as k:
                for c in range(1, 5):
                    step(k, c)
            for u in range(4 * whole + 1, units + 1):
                step(whole, u - 4 * whole)

        def is_unit(k, c):
            return not isinstance(k, int) or 0 <= 4 * k + c < units

        def rows_of(a, u):
            return a[bass.ds(u * UT, UT), :].rearrange("(p j) c -> p j c", j=J)

        @block.sync
        def _(sp):
            def load_x(k, c):
                wait(sp, sent[c % 4], 96 * (k + c // 4))
                sp.dma_start(x[c % 4][:, :, :], rows_of(x2_rows, 4 * k + c)).then_inc(x_in[c % 4], 16)

            def step(k, c):
                u = 4 * k + c
                if is_unit(k, c + 2):
                    load_x(k, c + 2)
                if is_unit(k, c + 1):
                    wait(sp, hs_ready, u)
                    sp.dma_start(hres[(c + 1) % 2][:, :, :], rows_of(h1_rows, u + 1)).then_inc(res_in[(c + 1) % 2], 16)
                if is_unit(k, c - 1):
                    i = (c - 1) % 2
                    sp.wait_ge(hs_ready, u)
                    sp.dma_start(rows_of(hs_rows, u - 1), hs[i][:, :, :]).then_inc(hs_st[i], 16)
                    sp.wait_ge(weight_ready, u)
                    sp.dma_start(weight_out[u - 1, :, :], weight[i][:, :, :].rearrange("p k j -> p (k j)")).then_inc(meta_st[i], 16)
                    sp.wait_ge(pos_ready, u)
                    sp.dma_start(pos_out[u - 1, :, :], posf[i][:, :, :].rearrange("p k j -> p (k j)")).then_inc(meta_st[i], 16)

            load_x(0, 0)
            for dst, src in ((wup[:, :, :], w_fc.rearrange("(k p) n -> p k n", p=KC)),
                             (wdn[:, :, :], w_pr.rearrange("(k p) n -> p k n", p=KC)),
                             (rt[:, :, :], router_t.rearrange("(k p) e -> p k e", p=KC)),
                             (bal[:, :], bias.rearrange("(o e) -> o e", o=1).to_broadcast([128, E]))):
                sp.dma_start(dst, src).then_inc(w_in, 16)
            steps(sp, step)
            sp.wait_ge(dconsts, DCONSTS)
            for n in range(E * SLOTS // 128):
                sp.dma_start(slots[E * REGION + n * 128:E * REGION + (n + 1) * 128, :], zrow[:, :]).then_inc(tail_st, 16)
            sp.wait_ge(tiles_ready, 1)
            sp.dma_start(tiles_out.rearrange("(o a) t -> o a t", o=1), tile_i[0:1, :, :]).then_inc(tiles_st, 16)
            sp.dma_start(steps_out, step_e[:, :]).then_inc(tiles_st, 16)
            sp.wait_ge(tiles_st, 32)
            sp.wait_ge(tail_st, 16 * (E * SLOTS // 128))
            for i in range(2):
                n = (units + 1 - i) // 2
                sp.wait_ge(hs_st[i], 16 * n)
                sp.wait_ge(meta_st[i], 32 * n)

        @block.gpsimd
        def _(pool):
            make_identity(nc, ident[:, :], 128, zeroed, consts)
            pool.memset(before[:, :], 1.0).then_inc(zeroed, 1)
            pool.wait_ge(zeroed, 2)
            pool.affine_select(out=before[:, :], in_=before[:, :], compare_op=ALU.is_gt, fill=0.0, base=0,
                               pattern=[[1, 128]], channel_multiplier=-1).then_inc(consts, 1)
            pool.iota(eid[:, :, :], pattern=[[0, J], [1, E]], base=0, channel_multiplier=0,
                      allow_small_or_imprecise_dtypes=True).then_inc(consts, 1)
            pool.iota(start[0][:, 0, :], pattern=[[REGION, E]], base=0, channel_multiplier=0,
                      allow_small_or_imprecise_dtypes=True).then_inc(consts, 1)
            pool.iota(lane[:, :], pattern=[[128, 2]], base=0, channel_multiplier=1,
                      allow_small_or_imprecise_dtypes=True).then_inc(consts, 1)
            pool.iota(grid[:, :, :], pattern=[[0, E], [SLOTS, MOST]], base=0, channel_multiplier=0,
                      allow_small_or_imprecise_dtypes=True).then_inc(consts, 1)
            pool.iota(tnum[:, :, :], pattern=[[1, NT], [0, E]], base=0, channel_multiplier=0,
                      allow_small_or_imprecise_dtypes=True).then_inc(consts, 1)

            def step(k, c):
                u = 4 * k + c
                if is_unit(k, c - 1):
                    i = (c - 1) % 4
                    pool.wait_ge(x_in[i], 16 * (k + (c - 1) // 4 + 1))
                    pool.wait_ge(pos_ready, u)
                    pool.sem_inc(units_begun, 1)
                    for n in range(2):
                        for j in range(J):
                            pool.indirect_dma_start(slots, bass.IndirectOffsetOnAxis(ap=posi[i % 2][:, n, j:j + 1], axis=0),
                                                    x[i][:, j, :], None).then_inc(sent[i], 16)
            steps(pool, step)
            pool.wait_ge(pad_ready, 1)
            pool.wait_ge(dconsts, DCONSTS)
            for n in range(2 * E):
                pool.indirect_dma_start(slots, bass.IndirectOffsetOnAxis(ap=padi[:, n:n + 1], axis=0), zrow[:, :], None)\
                    .then_inc(pad_sent, 16)
            pool.wait_ge(pad_sent, 32 * E)
            for i in range(4):
                pool.wait_ge(sent[i], 96 * ((units + 3 - i) // 4))

        @block.tensor
        def _(pe):
            pe.wait_ge(consts, CONSTS)
            pe.wait_ge(dconsts, DCONSTS)
            pe.wait_ge(w_in, LOADS)

            def step(k, c):
                u = 4 * k + c
                nxt, cur, prev = is_unit(k, c + 1), is_unit(k, c), is_unit(k, c - 1)
                if cur:
                    pe.wait_ge(xT_ev, u + 1)
                    for m in range(2):
                        wait(pe, sq_done, 2 * u - 1 + m)
                        for cc in range(2):
                            last = pe.matmul(hp[0:KC, m, 0:UT], wup[:, cc, m * KC:(m + 1) * KC], xT[:, cc, :],
                                             start=(cc == 0), stop=(cc == 1))
                        last.then_inc(up_mm, 1)
                    wait(pe, exp_ev, u)
                    for j in range(J):
                        for cc in range(2):
                            last = pe.matmul(lp[:, j * E:(j + 1) * E], xT[:, cc, j * 128:(j + 1) * 128], rt[:, cc, :],
                                             start=(cc == 0), stop=(cc == 1))
                    last.then_inc(lg_mm, 1)
                if nxt:
                    pe.wait_ge(x_in[(c + 1) % 4], 16 * (k + (c + 1) // 4 + 1))
                    wait(pe, xT_ev, u + 1)
                    for cc in range(2):
                        for j in range(J):
                            last = pe.transpose(tp[0:KC, cc, j * 128:(j + 1) * 128], x[(c + 1) % 4][:, j, cc * KC:(cc + 1) * KC],
                                                ident[:, :])
                    last.then_inc(x_tr, 1)
                if prev:
                    pe.wait_ge(mask_ready, u)
                    wait(pe, pos_ready, u - 1)
                    m = mask[(c - 1) % 2][:, :, :].rearrange("p j e -> p (j e)")
                    pe.matmul(rp[:, 0:J * E], before[:, :], m, start=True, stop=True)
                    pe.matmul(rp[:, J * E:2 * J * E], ones[:, :], m, start=True, stop=True).then_inc(rk_mm, 1)
                if cur:
                    wait(pe, hs_ready, u)
                    pe.wait_ge(sq_done, 2 * u + 2)
                    for j in range(J):
                        for cc in range(2):
                            last = pe.matmul(yp[:, j, 0:CH], hT[:, cc, j * 128:(j + 1) * 128], wdn[:, cc, :],
                                             start=(cc == 0), stop=(cc == 1))
                    last.then_inc(dn_mm, 1)
            steps(pe, step)

        @block.scalar
        def _(act):
            def step(k, c):
                u = 4 * k + c
                nxt, cur = is_unit(k, c + 1), is_unit(k, c)
                if cur:
                    for m in range(2):
                        act.wait_ge(up_mm, 2 * u + 1 + m)
                        act.activation(relu[:, m, :], hp[0:KC, m, 0:UT], ACT.Relu).then_inc(relu_ev, 1)
                        wait(act, dn_mm, u)
                        act.wait_ge(relu_ev, 2 * u + 1 + m)
                        act.activation(hT[:, m, :], relu[:, m, :], ACT.Square).then_inc(sq_done, 1)
                    act.wait_ge(lg_mm, u + 1)
                    wait(act, route, ROUTE * u)
                    act.activation(expo[:, :, :].rearrange("p j e -> p (j e)"), logits, ACT.Exp, scale=-1.0).then_inc(exp_ev, 1)
                if nxt:
                    act.wait_ge(x_tr, u + 2)
                    wait(act, lg_mm, u + 1)
                    act.activation(xT[:, :, :], tp[0:KC, :, 0:UT], ACT.Copy).then_inc(xT_ev, 1)
            steps(act, step)

        @block.vector
        def _(dve):
            dve.memset(ones[:, :], 1.0).then_inc(dconsts, 1)
            dve.memset(zrow[:, :], 0.0).then_inc(dconsts, 1)
            dve.memset(zeros_e[:, :], 0.0).then_inc(dconsts, 1)
            dve.memset(carrier[:, :], 0.0).then_inc(dconsts, 1)
            dve.wait_ge(consts, CONSTS)
            dve.wait_ge(w_in, LOADS)

            def chain(sem_, before_):
                done = [0]

                def then(instruction):
                    done[0] += 1
                    instruction.then_inc(sem_, 1)
                    dve.wait_ge(sem_, before_ + done[0])
                return then

            def over_k(a):
                return a.rearrange("p (o j) e -> p o j e", o=1).to_broadcast([128, 2, J, E])

            def choose(k, c):
                u, i = 4 * k + c, c % 2
                dve.wait_ge(exp_ev, u + 1)
                then = chain(route, ROUTE * u)
                then(dve.tensor_scalar(expo[:, :, :], expo[:, :, :], 1.0, None, ALU.add))
                then(dve.reciprocal(sig[:, :, :], expo[:, :, :]))
                then(dve.tensor_tensor(sel[:, :, :], sig[:, :, :],
                                       bal[:, :].rearrange("p (o e) -> p o e", o=1).to_broadcast([128, J, E]), ALU.add))
                dve.memset(carrier[:, :], 0.0)
                for j in range(J):
                    last = dve.max(top[:, j, :], sel[:, j, :])
                then(last)
                dve.memset(carrier[:, :], 0.0)
                for j in range(J):
                    last = dve.max_index(topi[:, j, :], top[:, j, :], sel[:, j, :])
                then(last)
                wait(dve, pos_ready, u - 1)
                for n in range(2):
                    last = dve.tensor_tensor(pick[i][:, n, :, :], topi[:, :, n:n + 1].to_broadcast([128, J, E]), eid[:, :, :],
                                             ALU.is_equal)
                then(last)
                wait(dve, rk_mm, u - 1)
                dve.tensor_tensor(mask[i][:, :, :], pick[i][:, 0, :, :], pick[i][:, 1, :, :], ALU.add).then_inc(mask_ready, 1)
                then(dve.tensor_tensor(prod[:, :, :, :], pick[i][:, :, :, :], over_k(sig[:, :, :]), ALU.mult))
                then(dve.tensor_reduce(chosen[:, :, :], prod[:, :, :, :], AXX, ALU.add))
                then(dve.tensor_tensor(wsum[:, :], chosen[:, 0, :], chosen[:, 1, :], ALU.add))
                then(dve.tensor_scalar(wsum[:, :], wsum[:, :], 1e-20, None, ALU.add))
                then(dve.reciprocal(wsum[:, :], wsum[:, :]))
                wait(dve, meta_st[i], 32 * (2 * k + c // 2))
                last = dve.tensor_tensor(weight[i][:, :, :], chosen[:, :, :],
                                         wsum[:, :].rearrange("p (o j) -> p o j", o=1).to_broadcast([128, 2, J]), ALU.mult)
                last.then_inc(weight_ready, 1)

            def find_rows(k, c):
                u, i = 4 * k + c, c % 2
                dve.wait_ge(rk_mm, u + 1)
                then = chain(place, PLACE * u)
                for j in range(1, J):
                    then(dve.tensor_tensor(start[i][:, j, :], start[i][:, j - 1, :], total[:, j - 1, :], ALU.add))
                then(dve.tensor_tensor(start[1 - i][:, 0, :], start[i][:, J - 1, :], total[:, J - 1, :], ALU.add))
                then(dve.tensor_tensor(rows[:, :, :], rank, start[i][:, :, :], ALU.add))
                then(dve.tensor_tensor(prod2[:, :, :, :], pick[i][:, :, :, :], over_k(rows[:, :, :]), ALU.mult))
                wait(dve, meta_st[i], 32 * (2 * k + c // 2))
                dve.tensor_reduce(posf[i][:, :, :], prod2[:, :, :, :], AXX, ALU.add).then_inc(summed, 1)
                wait(dve, sent[(c - 2) % 4], 96 * (k + (c - 2) // 4 + 1))
                dve.wait_ge(summed, u + 1)
                dve.tensor_copy(posi[i][:, :, :], posf[i][:, :, :]).then_inc(pos_ready, 1)

            def step(k, c):
                u = 4 * k + c
                if is_unit(k, c):
                    choose(k, c)
                if is_unit(k, c - 1):
                    find_rows(k, c - 1)
                if is_unit(k, c):
                    dve.wait_ge(dn_mm, u + 1)
                    dve.wait_ge(res_in[c % 2], 16 * (2 * k + c // 2 + 1))
                    wait(dve, hs_st[c % 2], 16 * (2 * k + c // 2))
                    dve.tensor_tensor(hs[c % 2][:, :, :], yp[:, 0:J, 0:CH], hres[c % 2][:, :, :], ALU.add).then_inc(hs_ready, 1)
            steps(dve, step)

            final = start[units % 2]
            then = chain(plan, 0)
            for n in range(2):
                last = dve.tensor_scalar(padf[:, n, :], final[:, 0, :], lane[:, n:n + 1], None, ALU.add)
            then(last)
            dve.tensor_copy(padi[:, :], padf[:, :, :].rearrange("p n e -> p (n e)")).then_inc(pad_ready, 1)
            then(dve.scalar_tensor_tensor(count[:, :], eid[:, 0, :], -float(REGION), final[:, 0, :], ALU.mult, ALU.add))
            then(dve.tensor_tensor(over[:, :, :], count[:, :].rearrange("o (e j) -> o e j", j=1).to_broadcast([128, E, MOST]),
                                   grid[:, :, :], ALU.is_gt))
            then(dve.tensor_reduce(ntile[:, :], over[:, :, :], AXX, ALU.add))
            then(dve.tensor_tensor_scan(ends[:, :], ntile[:, :], zeros_e[:, :], 0.0, ALU.add, ALU.add))
            then(dve.tensor_scalar(step_e[:, :], ntile[:, :], -float(SLOTS), float(REGION), ALU.mult, ALU.add))
            wide = lambda a: a.rearrange("o (t e) -> o t e", t=1).to_broadcast([128, NT, E])
            then(dve.tensor_tensor(past[:, :, :], tnum[:, :, :], wide(ends[:, :]), ALU.is_ge))
            then(dve.tensor_tensor(skip[:, :, :], past[:, :, :], wide(step_e[:, :]), ALU.mult))
            then(dve.tensor_reduce(tbase[:, :], skip[:, :, :], AXX, ALU.add))
            then(dve.tensor_reduce(texp[:, :], past[:, :, :], AXX, ALU.add))
            then(dve.scalar_tensor_tensor(tbase[:, :], tnum[:, :, 0], float(SLOTS), tbase[:, :], ALU.mult, ALU.add))
            then(dve.tensor_scalar(texp[:, :], texp[:, :], float(E - 1), None, ALU.min))
            dve.tensor_copy(tile_i[:, 0, :], tbase[:, :])
            dve.tensor_copy(tile_i[:, 1, :], texp[:, :]).then_inc(tiles_ready, 1)


def routed_experts(nc, slots, tiles, w_experts, y_slots):
    NT, E = tiles.shape[1], w_experts.shape[0]
    R, I = 4, SLOTS // 128
    I32 = mybir.dt.int32
    rows_max = slots.shape[0] - SLOTS
    with ExitStack() as ctx:
        sb = lambda name, shape, dt=F32: ctx.enter_context(nc.sbuf_tensor(name, shape, dt))
        sem = lambda name: ctx.enter_context(nc.semaphore(name))
        pb = lambda name, shape: ctx.enter_context(nc.psum_tensor(name, shape, F32))
        ident = sb("ident_x", [128, 128])
        tile_i = sb("tile_x", [1, 2, NT], I32)
        x = [sb(f"x_x{i}", [128, I, CH]) for i in range(R)]
        w = [sb(f"w_x{i}", [KC, 2, 2, CH]) for i in range(R)]
        xT = [sb(f"xT_x{i}", [KC, 2, SLOTS]) for i in range(2)]
        relu = [sb(f"relu_x{i}", [KC, 2, SLOTS]) for i in range(2)]
        hT = [sb(f"hT_x{i}", [KC, 2, SLOTS]) for i in range(2)]
        y = [sb(f"y_x{i}", [128, I, CH]) for i in range(R)]
        tp = [pb(f"tp_x{i}", [128, 2, SLOTS]) for i in range(2)]
        hp = [pb(f"hp_x{i}", [128, 2, SLOTS]) for i in range(2)]
        yp = [pb(f"yp_x{i}", [128, I, 256]) for i in range(2)]
        zeroed, consts, tiles_in = sem("zeroed_x"), sem("consts_x"), sem("tiles_in")
        x_in = [sem(f"x_in_x{i}") for i in range(R)]
        w_in = [sem(f"w_in_x{i}") for i in range(R)]
        y_st = [sem(f"y_st{i}") for i in range(R)]
        x_tr, xT_ev, up_mm, relu_ev, sq_done, dn_mm, y_ev = (
            sem(n) for n in ("x_tr_x", "xT_ev_x", "up_mm_x", "relu_ev_x", "sq_done_x", "dn_mm_x", "y_ev"))
        block = ctx.enter_context(nc.Block())

        def steps(eng, step, first=-2):
            whole = (NT - 5) // R
            for c in range(first, 1):
                step(0, c)
            with eng.Fori(0, whole) as k:
                for c in range(1, 1 + R):
                    step(k, c)
            for t in range(R * whole + 1, NT):
                step(whole, t - R * whole)

        def is_tile(k, c):
            return not isinstance(k, int) or 0 <= R * k + c < NT

        @block.gpsimd
        def _(pool):
            make_identity(nc, ident[:, :], 128, zeroed, consts)

        @block.sync
        def _(sp):
            sp.dma_start(tile_i[:, :, :], tiles.rearrange("(o a) t -> o a t", o=1)).then_inc(tiles_in, 16)
            sp.wait_ge(tiles_in, 16)

            def load(k, c):
                t, i = R * k + c, c % R
                row = sp.value_load(tile_i[0:1, 0, bass.ds(t, 1)], min_val=0, max_val=rows_max)
                e = sp.value_load(tile_i[0:1, 1, bass.ds(t, 1)], min_val=0, max_val=E - 1)
                wait(sp, x_tr, t + 1 - R)
                sp.dma_start(x[i][:, :, :], slots[bass.ds(row, SLOTS), :].rearrange("(p i) c -> p i c", i=I)).then_inc(x_in[i], 16)
                wait(sp, dn_mm, t + 1 - R)
                sp.dma_start(w[i][:, :, :, :], w_experts[bass.ds(e, 1), :, :, :, :].rearrange("o p w k n -> (o p) w k n"))\
                    .then_inc(w_in[i], 16)
            for c in range(R):
                load(0, c)

            def step(k, c):
                if is_tile(k, c + R):
                    load(k, c + R)
            steps(sp, step, first=0)

        @block.tensor
        def _(pe):
            pe.wait_ge(consts, 1)

            def step(k, c):
                t = R * k + c
                if is_tile(k, c + 2):
                    i = (c + 2) % R
                    pe.wait_ge(x_in[i], 16 * (k + (c + 2) // R + 1))
                    wait(pe, xT_ev, t + 1)
                    for cc in range(2):
                        for n in range(I):
                            last = pe.transpose(tp[c % 2][0:KC, cc, n * 128:(n + 1) * 128], x[i][:, n, cc * KC:(cc + 1) * KC], ident[:, :])
                    last.then_inc(x_tr, 1)
                if is_tile(k, c + 1):
                    i = (c + 1) % R
                    pe.wait_ge(w_in[i], 16 * (k + (c + 1) // R + 1))
                    pe.wait_ge(xT_ev, t + 2)
                    wait(pe, sq_done, t)
                    for m in range(2):
                        for cc in range(2):
                            last = pe.matmul(hp[(c + 1) % 2][0:KC, m, :], w[i][:, 0, cc, m * KC:(m + 1) * KC], xT[(c + 1) % 2][:, cc, :],
                                             start=(cc == 0), stop=(cc == 1))
                    last.then_inc(up_mm, 1)
                if is_tile(k, c):
                    pe.wait_ge(sq_done, t + 1)
                    wait(pe, y_ev, t - 1)
                    for n in range(I):
                        for cc in range(2):
                            last = pe.matmul(yp[c % 2][:, n, 0:CH], hT[c % 2][:, cc, n * 128:(n + 1) * 128], w[c % R][:, 1, cc, :],
                                             start=(cc == 0), stop=(cc == 1))
                    last.then_inc(dn_mm, 1)
            steps(pe, step)

        @block.vector
        def _(dve):
            def step(k, c):
                t = R * k + c
                if is_tile(k, c + 1):
                    i = (c + 1) % 2
                    dve.wait_ge(relu_ev, t + 2)
                    wait(dve, dn_mm, t)
                    dve.tensor_tensor(hT[i][:, :, :], relu[i][:, :, :], hp[i][0:KC, :, :], ALU.mult).then_inc(sq_done, 1)
                if is_tile(k, c):
                    dve.wait_ge(dn_mm, t + 1)
                    wait(dve, y_st[c % R], 16 * (k + c // R))
                    dve.tensor_copy(y[c % R][:, :, :], yp[c % 2][:, :, 0:CH]).then_inc(y_ev, 1)
            steps(dve, step)

        @block.scalar
        def _(act):
            def step(k, c):
                t = R * k + c
                if is_tile(k, c + 2):
                    act.wait_ge(x_tr, t + 3)
                    wait(act, up_mm, t + 1)
                    act.activation(xT[c % 2][:, :, :], tp[c % 2][0:KC, :, :], ACT.Copy).then_inc(xT_ev, 1)
                if is_tile(k, c + 1):
                    act.wait_ge(up_mm, t + 2)
                    wait(act, sq_done, t)
                    act.activation(relu[(c + 1) % 2][:, :, :], hp[(c + 1) % 2][0:KC, :, :], ACT.Relu).then_inc(relu_ev, 1)
                if is_tile(k, c):
                    act.wait_ge(y_ev, t + 1)
                    act.dma_start(y_slots[bass.ds(t * SLOTS, SLOTS), :].rearrange("(p i) c -> p i c", i=I), y[c % R][:, :, :])\
                        .then_inc(y_st[c % R], 16)
            steps(act, step)
            for i in range(R):
                act.wait_ge(y_st[i], 16 * ((NT + R - 1 - i) // R))


def combine_experts(nc, hs_rows, y_slots, pos, weight, steps_in, out_rows):
    T, J, E = hs_rows.shape[0], 3, steps_in.shape[1]
    UT = 128 * J
    units = T // UT
    REGION = region_rows(T)
    with ExitStack() as ctx:
        sb = lambda name, shape, dt=F32: ctx.enter_context(nc.sbuf_tensor(name, shape, dt))
        sem = lambda name: ctx.enter_context(nc.semaphore(name))
        hs = [sb(f"hs_c{i}", [128, J, CH]) for i in range(4)]
        y = [sb(f"y_c{i}", [128, 2, J, CH]) for i in range(4)]
        ps = [sb(f"pos_c{i}", [128, 2 * J]) for i in range(4)]
        ws = [sb(f"weight_c{i}", [128, 2, J]) for i in range(4)]
        yi = [sb(f"y_row{i}", [128, 2 * J], mybir.dt.int32) for i in range(4)]
        edge = sb("edge", [128, 2 * J, E - 1])
        gap = sb("gap", [128, E])
        past, off, gone = sb("past_c", [128, 2 * J, E - 1]), sb("off_c", [128, 2 * J, E - 1]), sb("gone", [128, 2 * J])
        units_begun, edges, gap_in, chain = sem("units_begun_c"), sem("edges"), sem("gap_in"), sem("locate")
        meta_in = [sem(f"meta_in{i}") for i in range(4)]
        hs_in = [sem(f"hs_in{i}") for i in range(4)]
        y_in = [sem(f"y_in{i}") for i in range(4)]
        out_st = [sem(f"out_st{i}") for i in range(4)]
        located, first, second = sem("located"), sem("first_added"), sem("second_added")
        block = ctx.enter_context(nc.Block())

        def steps(eng, step):
            for c in range(4):
                step(0, c)
            with eng.Fori(1, units // 4 - 1) as k:
                for c in range(4):
                    step(k, c)
            for c in range(4 + units % 4):
                step(units // 4 - 1, c)

        def rows_of(a, u):
            return a[bass.ds(u * UT, UT), :].rearrange("(p j) c -> p j c", j=J)

        @block.sync
        def _(sp):
            sp.dma_start(gap[:, :], steps_in).then_inc(gap_in, 16)

            def step(k, c):
                u, i = 4 * k + c, c % 4
                wait(sp, second, u - 3)
                sp.dma_start(ps[i][:, :], pos[u, :, :]).then_inc(meta_in[i], 16)
                sp.dma_start(ws[i][:, :, :].rearrange("p k j -> p (k j)"), weight[u, :, :]).then_inc(meta_in[i], 16)
                wait(sp, out_st[i], 16 * (k + c // 4))
                sp.dma_start(hs[i][:, :, :], rows_of(hs_rows, u)).then_inc(hs_in[i], 16)
            steps(sp, step)

        @block.gpsimd
        def _(pool):
            pool.iota(edge[:, :, :], pattern=[[0, 2 * J], [REGION, E - 1]], base=REGION, channel_multiplier=0,
                      allow_small_or_imprecise_dtypes=True).then_inc(edges, 1)

            def step(k, c):
                u, i = 4 * k + c, c % 4
                wait(pool, second, u - 3)
                pool.wait_ge(located, u + 1)
                pool.sem_inc(units_begun, 1)
                for n in range(2):
                    for j in range(J):
                        m = n * J + j
                        pool.indirect_dma_start(y[i][:, n, j, :], None, y_slots,
                                                bass.IndirectOffsetOnAxis(ap=yi[i][:, m:m + 1], axis=0)).then_inc(y_in[i], 16)
            steps(pool, step)

        @block.vector
        def _(dve):
            dve.wait_ge(edges, 1)
            dve.wait_ge(gap_in, 16)

            def locate(k, c):
                u, i = 4 * k + c, c % 4
                dve.wait_ge(meta_in[i], 32 * (k + c // 4) + 32)
                p = ps[i][:, :].rearrange("p (m e) -> p m e", e=1).to_broadcast([128, 2 * J, E - 1])
                g = gap[:, 0:E - 1].rearrange("p (m e) -> p m e", m=1).to_broadcast([128, 2 * J, E - 1])
                dve.tensor_tensor(past[:, :, :], p, edge[:, :, :], ALU.is_ge).then_inc(chain, 1)
                dve.wait_ge(chain, 3 * u + 1)
                dve.tensor_tensor(off[:, :, :], past[:, :, :], g, ALU.mult).then_inc(chain, 1)
                dve.wait_ge(chain, 3 * u + 2)
                dve.tensor_reduce(gone[:, :], off[:, :, :], AXX, ALU.add).then_inc(chain, 1)
                wait(dve, y_in[i], 96 * (k + c // 4))
                dve.wait_ge(chain, 3 * u + 3)
                dve.tensor_tensor(yi[i][:, :], ps[i][:, :], gone[:, :], ALU.subtract).then_inc(located, 1)

            def step(k, c):
                u, i = 4 * k + c, c % 4
                if not isinstance(k, int) or u + 2 < units:
                    locate(k, c + 2)
                dve.wait_ge(hs_in[i], 16 * (k + c // 4) + 16)
                dve.wait_ge(y_in[i], 96 * (k + c // 4) + 96)
                for n, done in ((0, first), (1, second)):
                    if n:
                        dve.wait_ge(first, u + 1)
                    for j in range(J):
                        last = dve.scalar_tensor_tensor(hs[i][:, j, :], y[i][:, n, j, :], ws[i][:, n, j:j + 1], hs[i][:, j, :],
                                                        ALU.mult, ALU.add)
                    last.then_inc(done, 1)
            for c in range(2):
                locate(0, c)
            steps(dve, step)

        @block.scalar
        def _(act):
            def step(k, c):
                u, i = 4 * k + c, c % 4
                act.wait_ge(second, u + 1)
                act.dma_start(rows_of(out_rows, u), hs[i][:, :, :]).then_inc(out_st[i], 16)
            steps(act, step)
            for c in range(4):
                act.wait_ge(out_st[c], 16 * ((units + 3 - c) // 4))


def program(nc, patches, w_tok, txt, w_qkv, w_proj, b_proj, w_fc, w_pr, w_experts, router_t, bias, out):
    B, N = out.shape[0], out.shape[1]
    h_img = nc.dram_tensor("h_img_dram", (patches.shape[0] * 128, CH), F32, kind="Internal").ap()
    h1 = nc.dram_tensor("h1_dram", (B * N, CH), F32, kind="Internal").ap()
    x2 = nc.dram_tensor("x2_dram", (B * N, CH), F32, kind="Internal").ap()
    embed_patches(nc, patches, w_tok, h_img)
    images = lambda a: a.rearrange("(b t p) c -> b p t c", t=2, p=N // 2)
    attention(nc, h_img, txt, w_qkv, w_proj, b_proj, images(h1), images(x2))
    T, E, units = B * N, router_t.shape[1], B * N // 384
    slot_rows = E * region_rows(T) + E * SLOTS
    tiles = -(-(2 * T + E * (SLOTS - 1)) // SLOTS)
    hs = nc.dram_tensor("hs_dram", (T, CH), F32, kind="Internal").ap()
    slots = nc.dram_tensor("slots_dram", (slot_rows, CH), F32, kind="Internal").ap()
    y_slots = nc.dram_tensor("y_slots_dram", (tiles * SLOTS, CH), F32, kind="Internal").ap()
    pos = nc.dram_tensor("pos_dram", (units, 128, 6), F32, kind="Internal").ap()
    gaps = nc.dram_tensor("gaps_dram", (128, E), F32, kind="Internal").ap()
    weight = nc.dram_tensor("weight_dram", (units, 128, 6), F32, kind="Internal").ap()
    tile_list = nc.dram_tensor("tile_list_dram", (2, tiles), mybir.dt.int32, kind="Internal").ap()
    shared_expert_and_routing(nc, x2, h1, w_fc, w_pr, router_t, bias, hs, slots, pos, weight, tile_list, gaps)
    routed_experts(nc, slots, tile_list, w_experts, y_slots)
    combine_experts(nc, hs, y_slots, pos, weight, gaps, out.rearrange("b n c -> (b n) c"))


def patch_columns(x):
    starts = np.clip(np.arange(GRID) * PATCH - OVERLAP, 0, IMG - WIN)
    idx = (starts[:, None] + np.arange(WIN)[None, :]).reshape(-1)
    B = x.shape[0]
    g = np.take(np.take(x, idx, axis=1), idx, axis=2).reshape(B, GRID, WIN, GRID, WIN, 3)
    g = g.transpose(0, 1, 3, 2, 4, 5).reshape(B * GRID * GRID // 128, 128, 12, 121)
    return np.ascontiguousarray(g.transpose(0, 3, 2, 1))


def expert_weights(w1, w2):
    w = np.stack([w1, w2], axis=1)
    return np.ascontiguousarray(w.reshape(w.shape[0], 2, 2, KC, CH).transpose(0, 3, 1, 2, 4))


def kernel(**inputs):
    import concourse.bacc as bacc
    from concourse.bass_utils import run_bass_kernel_spmd
    a = {n: np.asarray(v) for n, v in inputs.items()}
    B, n_txt = a["txt"].shape[:2]
    N = GRID * GRID + n_txt
    arrays = {
        "patches": patch_columns(a["x"]), "w_tok": a["L0_tok_W"], "txt": a["txt"],
        "w_qkv": a["L0_attn_Wqkv"], "w_proj": a["L0_attn_Wproj"], "b_proj": a["L0_attn_bproj"],
        "w_fc": a["L0_ffn_w_fc_sh"], "w_pr": a["L0_ffn_w_proj_sh"],
        "w_experts": expert_weights(a["L0_ffn_w1"], a["L0_ffn_w2"]),
        "router_t": np.ascontiguousarray(a["L0_ffn_router_w"].T), "bias": a["L0_ffn_balance_bias"],
    }
    nc = bacc.Bacc("TRN2", target_bir_lowering=False, num_devices=1)
    args = [nc.dram_tensor(n, v.shape, mybir.dt.from_np(v.dtype), kind="ExternalInput").ap() for n, v in arrays.items()]
    out = nc.dram_tensor("out_dram", (B, N, CH), F32, kind="ExternalOutput").ap()
    program(nc, *args, out)
    return run_bass_kernel_spmd(nc, [arrays], core_ids=[0]).results[0]["out_dram"]
```

```python
import numpy as np
import concourse.bass as bass
from concourse import mybir
from concourse.alu_op_type import AluOpType as ALU
from contextlib import ExitStack

F32 = mybir.dt.float32
F32R = mybir.dt.float32r
ACT = mybir.ActivationFunctionType
AXX = mybir.AxisListType.X

GRID, IMG, WIN, PATCH, OVERLAP = 14, 224, 22, 16, 3
CH = 192
KC = 96
HEADS, HD = 12, 16
AUX, GROUPS = 8, 4
EPS = 1e-5
SLOTS = 256
ROW = CH + 2


def wait(eng, sem, value):
    if isinstance(value, int) and value <= 0:
        return
    eng.wait_ge(sem, value)


def make_identity(nc, ident, n, zeroed, ready):
    nc.gpsimd.memset(ident, 0.0).then_inc(zeroed, 1)
    nc.gpsimd.wait_ge(zeroed, 1)
    nc.gpsimd.affine_select(out=ident, in_=ident, compare_op=ALU.not_equal, fill=1.0, base=0,
                            pattern=[[-1, n]], channel_multiplier=1).then_inc(ready, 1)


def embed_patches(nc, patches, w_tok, h_img):
    chunks, kp, kt, m = patches.shape
    RING = 7
    rounds = chunks // RING
    assert chunks == rounds * RING and m == 128
    with ExitStack() as ctx:
        sb = lambda name, shape, dt=F32: ctx.enter_context(nc.sbuf_tensor(name, shape, dt))
        sem = lambda name: ctx.enter_context(nc.semaphore(name))
        w = sb("w_tok_sb", [kp, kt, CH])
        w_parts = sb("w_tok_parts", [kp, kt, 2, CH], F32R)
        pat = [sb(f"pat{i}", [kp, kt, m]) for i in range(RING)]
        high = [sb(f"pat_high{i}", [kp, kt, m], F32R) for i in range(RING)]
        low = [sb(f"pat_low{i}", [kp, kt, m], F32R) for i in range(RING)]
        emb = [sb(f"emb{i}", [m, CH]) for i in range(RING)]
        ps = [ctx.enter_context(nc.psum_tensor(f"emb_ps{i}", [m, 2, CH], F32)) for i in range(RING)]
        w_in, w_high, w_ready = [sem(f"w_tok_in{n}") for n in range(2)], sem("w_high"), sem("w_ready")
        halves = (slice(0, kt // 2), slice(kt // 2, kt))
        pat_in = [sem(f"pat_in{i}") for i in range(RING)]
        emb_out = [sem(f"emb_out{i}") for i in range(RING)]
        high_ready, low_ready, emb_mm, emb_ev = sem("high_ready"), sem("low_ready"), sem("emb_mm"), sem("emb_ev")
        block = ctx.enter_context(nc.Block())

        def steps(eng, step):
            for k in range(2):
                for i in range(RING):
                    step(k, i)
            with eng.Fori(2, rounds) as k:
                for i in range(RING):
                    step(k, i)

        @block.sync
        def _(sp):
            def load(k, i):
                wait(sp, low_ready, k * RING + i + 1 - RING)
                sp.dma_start(pat[i][:, :, :], patches[k * RING + i, :, :, :]).then_inc(pat_in[i], 16)
            for n, half in enumerate(halves):
                sp.dma_start(w[:, half, :], w_tok.rearrange("(t p) c -> p t c", p=kp)[:, half, :]).then_inc(w_in[n], 16)
            steps(sp, load)

        @block.tensor
        def _(pe):
            def chunk(k, i):
                pe.wait_ge(low_ready, k * RING + i + 1)
                wait(pe, emb_ev, k * RING + i + 1 - RING)
                for t in range(kt):
                    if isinstance(k, int) and k == i == 0 and t == kt // 2:
                        pe.wait_ge(w_ready, 2)
                    pe.matmul(ps[i][:, :, :].rearrange("p a c -> p (a c)"), high[i][:, t, :],
                              w_parts[:, t, :, :].rearrange("p a c -> p (a c)"), start=(t == 0), stop=False)
                    last = pe.matmul(ps[i][:, 0, :], low[i][:, t, :], w_parts[:, t, 0, :], start=False, stop=(t == kt - 1))
                last.then_inc(emb_mm, 1)
            pe.wait_ge(w_ready, 1)
            steps(pe, chunk)

        @block.vector
        def _(dve):
            def evacuate(k, i):
                dve.wait_ge(emb_mm, k * RING + i + 1)
                wait(dve, emb_out[i % RING], 16 * (k + i // RING))
                dve.tensor_reduce(emb[i % RING][:, :], ps[i % RING][:, :, :].rearrange("p a c -> p c a"), AXX, ALU.add)\
                   .then_inc(emb_ev, 1)

            def chunk(k, i):
                dve.wait_ge(high_ready, k * RING + i + 1)
                wait(dve, emb_mm, k * RING + i + 1 - RING)
                dve.tensor_tensor(low[i][:, :, :], pat[i][:, :, :], high[i][:, :, :], ALU.subtract).then_inc(low_ready, 1)
                if not isinstance(k, int) or k * RING + i >= 2:
                    evacuate(k, i - 2)
            for n, half in enumerate(halves):
                dve.wait_ge(w_high, n + 1)
                dve.tensor_tensor(w_parts[:, half, 1, :], w[:, half, :], w_parts[:, half, 0, :], ALU.subtract).then_inc(w_ready, 1)
            steps(dve, chunk)
            for i in (RING - 2, RING - 1):
                evacuate(rounds - 1, i)

        @block.scalar
        def _(act):
            def store(k, i):
                act.wait_ge(emb_ev, k * RING + i + 1)
                act.dma_start(h_img[bass.ds((k * RING + i) * m, m), :], emb[i % RING][:, :]).then_inc(emb_out[i % RING], 16)

            def chunk(k, i):
                act.wait_ge(pat_in[i], 16 * k + 16)
                wait(act, emb_mm, k * RING + i + 1 - RING)
                act.activation(high[i][:, :, :], pat[i][:, :, :], ACT.Copy).then_inc(high_ready, 1)
                if not isinstance(k, int) or k * RING + i >= 5:
                    store(k, i - 5)
            for n, half in enumerate(halves):
                act.wait_ge(w_in[n], 16)
                act.activation(w_parts[:, half, 0, :], w[:, half, :], ACT.Copy).then_inc(w_high, 1)
            steps(act, chunk)
            for i in range(RING - 5, RING):
                store(rounds - 1, i)
            for i in range(RING):
                act.wait_ge(emb_out[i], 16 * rounds)


def region_rows(T):
    return T + SLOTS


def attention_and_routing(nc, h_img, txt, w_qkv, w_proj, b_proj, router_t, bias,
                          h1_out, x2_out, slots, w_out, tile_i, texp):
    B, n_txt = txt.shape[0], txt.shape[1]
    n_img = h_img.shape[0] // B
    N = n_img + n_txt
    HT = N // 2
    INNER = (N - AUX) // GROUPS
    KEYS = AUX + INNER
    SL = 64
    HC = KC // HD
    PAIRS = HEADS // 2
    VW = 48
    T, E, J = B * N, router_t.shape[1], 2
    REGION = region_rows(T)
    NT = tile_i.shape[2]
    MOST = -(-T // SLOTS)
    I32, BF16 = mybir.dt.int32, mybir.dt.bfloat16
    assert B % 4 == 0 and B >= 12 and n_img % 2 == 0 and AUX % 2 == 0 and 2 * HT == N and KEYS == SL - 1
    with ExitStack() as ctx:
        sb = lambda name, shape, dt=F32: ctx.enter_context(nc.sbuf_tensor(name, shape, dt))
        sem = lambda name: ctx.enter_context(nc.semaphore(name))
        pb = lambda name, shape: ctx.enter_context(nc.psum_tensor(name, shape, F32))
        ident = sb("ident_a", [128, 128])
        wqkv = sb("wqkv_sb", [KC, 2, 3 * CH])
        wproj = sb("wproj_sb", [KC + 1, 2, CH])
        mask = sb("head_mask", [KC, HC])
        h = [sb(f"h_sb{i}", [HT, 2, CH]) for i in range(4)]
        stats, mv = sb("stats", [HT, 2, 6]), sb("mv", [HT, 2, 2])
        vare, rstd = sb("vare", [HT, 2]), sb("rstd", [HT, 2])
        stats2, mv2 = sb("stats2", [HT, 2, 6]), sb("mv2", [HT, 2, 2])
        vare2, rstd2 = sb("vare2", [HT, 2]), sb("rstd2", [HT, 2])
        mhalf, eps = sb("minus_half", [HT, 2]), sb("eps", [HT, 2])
        carrier = sb("carrier", [HT, 1])
        xn = sb("xn", [HT, 2, CH])
        xT = sb("xT", [KC, 2, GROUPS, SL])
        qT = sb("qT", [KC, 2, GROUPS * SL])
        kT = sb("kT", [KC, 2 * GROUPS, SL])
        kbd = sb("kbd", [KC, 2 * GROUPS, HC, SL])
        vbd = [sb(f"vbd{i}", [128, 2, PAIRS, 2, VW]) for i in range(2)]
        prob = [sb(f"prob{t}", [128, HEADS, SL]) for t in range(2)]
        rmax = sb("rowmax", [128, 2, HEADS])
        pT = [sb(f"pT{t}", [128, PAIRS, 128]) for t in range(2)]
        rden = sb("rden", [128, 2, PAIRS, 2])
        o = sb("o", [128, 2, CH])
        oT = sb("oT", [KC + 1, 2, N])
        auxp = sb("auxp", [KC, 2, GROUPS, AUX])
        auxs = sb("auxs", [KC, 2, AUX])
        h1 = [sb(f"h1_{i}", [HT, 2, CH]) for i in range(2)]
        x2 = [sb(f"x2_{i}", [HT, 2, ROW]) for i in range(4)]
        before = sb("before", [HT, 128], BF16)
        ones = sb("ones_r", [HT, 128], BF16)
        rt = sb("router_sb", [KC, 2, E])
        bal = sb("balance_sb", [HT, E])
        eid = sb("eid", [128, J, E])
        x2T = sb("x2T", [KC, 2, N])
        expo, sig, sel = (sb(n, [HT, J, E]) for n in ("expo", "sig", "sel"))
        top = sb("top", [HT, J, 8])
        topi = sb("topi", [HT, J, 8], mybir.dt.uint32)
        pick = [sb(f"pick{i}", [HT, 2, J, E]) for i in range(2)]
        mask2 = [sb(f"mask{i}", [HT, J, E], BF16) for i in range(2)]
        prod, prod2 = sb("prod", [HT, 2, J, E]), sb("prod2", [HT, 2, J, E])
        chosen = sb("chosen", [HT, 2, J])
        wsum = sb("wsum", [HT, J])
        meta = [sb(f"meta{i}", [HT, 4, J]) for i in range(4)]
        start = [sb(f"start{i}", [128, J, E]) for i in range(2)]
        rows = sb("rows", [HT, J, E])
        posi = [sb(f"posi{i}", [HT, 2, J], I32) for i in range(2)]
        zrow = sb("zrow", [128, SLOTS // 128, CH])
        nobody = sb("nobody", [128, 2 * E, SLOTS // 128, 2])
        per_image = sb("per_image", [HT, J])
        count = sb("count", [128, E])
        grid, over = sb("grid", [128, E, MOST]), sb("over", [128, E, MOST])
        ntile, ends, step_e, zeros_e = (sb(n, [128, E]) for n in ("ntile", "ends", "step_e", "zeros_e"))
        tnum = sb("tnum", [128, NT, E])
        past, skip = sb("past", [128, NT, E]), sb("skip", [128, NT, E])
        tbase = sb("tbase", [128, NT])
        last_row = sb("last_row", [1, E], I32)
        sc = [pb(f"sc{t}", [128, 2, 512]) for t in range(2)]
        px = pb("px", [128, 512])
        pw = pb("pw", [128, 512])
        pyz = pb("pyz", [128, 8, 128])
        x_v = px[0:KC, 0:2 * N].rearrange("p (c n) -> p c n", c=2)
        k_v = px[0:KC, :]
        v_v = px[:, 0:2 * CH].rearrange("p (t c) -> p t c", t=2)
        ot_v = pw[0:KC, :].rearrange("p (c n) -> p c n", c=2)
        q_v = pw[0:KC, :]
        x2t_v = sc[0][0:KC, 0, 0:2 * N].rearrange("p (c n) -> p c n", c=2)
        lg_v = sc[1][0:HT, 0, 0:J * E]
        rank_v = sc[1][0:HT, 1, 0:J * E].rearrange("p (j e) -> p j e", j=J)
        total_v = sc[1][:, 1, J * E:2 * J * E].rearrange("p (j e) -> p j e", j=J)
        pr_v = pw[0:HT, 0:2 * CH].rearrange("p (t c) -> p t c", t=2)

        zeroed, consts, const_in = sem("zeroed_a"), sem("consts_a"), sem("const_in")
        values_zeroed, ones_set = sem("values_zeroed"), sem("ones_set")
        h_in = [sem(f"h_in{i}") for i in range(4)]
        ln_stats, ln_mv, ln_var, ln_rstd, xn_ready = (sem(n) for n in ("ln_stats", "ln_mv", "ln_var", "ln_rstd", "xn_ready"))
        ln2_stats, ln2_mv, ln2_var, ln2_rstd, x2_ready = (sem(n) for n in ("ln2_stats", "ln2_mv", "ln2_var", "ln2_rstd", "x2_ready"))
        xT_mm, q_mm, k_mm, v_mm, s_mm, pt_mm, av_mm, ot_mm, proj_mm = (
            sem(n) for n in ("xT_mm", "q_mm", "k_mm", "v_mm", "s_mm", "pt_mm", "av_mm", "ot_mm", "proj_mm"))
        xT_ev, q_ev, k_ev, v_ev, pt_ev, exp_done, ot_ev = (
            sem(n) for n in ("xT_ev", "q_ev", "k_ev", "v_ev", "pt_ev", "exp_done", "ot_ev"))
        kbd_ready, rmax_ready, sub_done, rden_ready, av_ev, aux_sum, aux_ready, h1_ready = (
            sem(n) for n in ("kbd_ready", "rmax_ready", "sub_done", "rden_ready", "av_ev", "aux_sum", "aux_ready", "h1_ready"))
        h1_st = [sem(f"h1_st{i}") for i in range(2)]
        x2_st = [sem(f"x2_st{i}") for i in range(4)]
        sent = [sem(f"sent{i}") for i in range(4)]
        meta_st = [sem(f"meta_st{i}") for i in range(4)]
        kT_ready = sem("kT_ready")
        x2_tr, x2T_ev, lg_mm, exp_ev, rk_mm = (sem(n) for n in ("x2_tr", "x2T_ev", "lg_mm", "exp_ev", "rk_mm"))
        applied = sem("applied")
        route, mask_ready, weight_ready, place, summed, pos_ready, images_sent = (
            sem(n) for n in ("route", "mask_ready", "weight_ready", "place", "summed", "pos_ready", "images_sent"))
        plan, pad_ready, pad_sent, tail_st = (sem(n) for n in ("plan", "pad_ready", "pad_sent", "tail_st"))
        block = ctx.enter_context(nc.Block())
        CONSTS = 20
        ROUTE, PLACE = 11, 4

        def steps(eng, step):
            for c in range(-2, 7):
                step(0, c)
            with eng.Fori(1, (B - 8) // 4) as k:
                for u in range(4):
                    step(k, 3 + u)
            for c in range(3, 11):
                step((B - 8) // 4, c)

        def pad(eng, experts):
            eng.wait_ge(pad_ready, 1)
            for e in experts:
                row = eng.value_load(last_row[0:1, e:e + 1], min_val=e * REGION, max_val=e * REGION + T)
                zero_rows(eng, row, e, pad_sent)

        def zero_rows(eng, row, n, sent_):
            to = slots[bass.ds(row, SLOTS), :].rearrange("(p i) c -> p i c", i=SLOTS // 128)
            eng.dma_start(to[:, :, 0:CH], zrow[:, :, :]).then_inc(sent_, 16)
            eng.dma_start(to[:, :, CH:ROW], nobody[:, n, :, :]).then_inc(sent_, 16)

        def is_image(k, c):
            return not isinstance(k, int) or 0 <= 4 * k + c < B

        @block.sync
        def _(sp):
            def load(k, c):
                b, r = 4 * k + c, c % 4
                sp.dma_start(h[r][0:n_img // 2, :, :], h_img[bass.ds(b * n_img, n_img), :].rearrange("(p t) c -> p t c", t=2))\
                  .then_inc(h_in[r], 16)
                sp.dma_start(h[r][n_img // 2:HT, :, :], txt[b, :, :].rearrange("(p t) c -> p t c", t=2)).then_inc(h_in[r], 16)

            def step(k, c):
                s = 4 * k + c
                if is_image(k, c - 1):
                    sp.wait_ge(h1_ready, s)
                    sp.dma_start(h1_out[s - 1, :, :, :], h1[(c - 1) % 2][:, :, :]).then_inc(h1_st[(c - 1) % 2], 16)
                if c + 3 >= 4 and is_image(k, c + 3):
                    load(k, c + 3)
                if is_image(k, c - 1):
                    sp.wait_ge(x2_ready, s)
                    sp.dma_start(x2_out[s - 1, :, :, :], x2[(c - 1) % 4][:, :, 0:CH]).then_inc(x2_st[(c - 1) % 4], 16)
                if is_image(k, c - 3):
                    sp.wait_ge(weight_ready, s - 2)
                    sp.dma_start(w_out[:, s - 3, :, :].rearrange("m p t -> p m t"), meta[(c - 3) % 4][:, 2:4, :])\
                      .then_inc(meta_st[(c - 3) % 4], 16)

            load(0, 0)
            sp.dma_start(wqkv[:, :, :], w_qkv.rearrange("(k p) n -> p k n", p=KC)).then_inc(const_in, 16)
            for b in range(1, 4):
                load(0, b)
            sp.dma_start(wproj[0:KC, :, :], w_proj.rearrange("(k p) n -> p k n", p=KC)).then_inc(const_in, 16)
            sp.dma_start(wproj[KC:KC + 1, 0, :], b_proj.rearrange("(a n) -> a n", a=1)).then_inc(const_in, 16)
            sp.dma_start(rt[:, :, :], router_t.rearrange("(k p) e -> p k e", p=KC)).then_inc(const_in, 16)
            sp.dma_start(bal[:, :], bias.rearrange("(o e) -> o e", o=1).to_broadcast([HT, E])).then_inc(const_in, 16)
            steps(sp, step)
            pad(sp, range(0, E, 2))
            sp.wait_ge(pad_sent, 32 * E)
            sp.wait_ge(tail_st, 32 * E)
            for i in range(2):
                sp.wait_ge(h1_st[i], 16 * (B // 2))
            for i in range(4):
                sp.wait_ge(x2_st[i], 16 * (B // 4))
                sp.wait_ge(meta_st[i], 16 * (B // 4))

        @block.gpsimd
        def _(pool):
            make_identity(nc, ident[:, :], 128, zeroed, consts)
            pool.memset(mhalf[:, :], -0.5).then_inc(consts, 1)
            pool.memset(eps[:, :], EPS).then_inc(consts, 1)
            pool.memset(per_image[:, :], 2.0 * N).then_inc(consts, 1)
            pool.memset(nobody[:, :, :, 1], -1.0).then_inc(consts, 1)
            pool.memset(mask[:, :], 1.0).then_inc(zeroed, 1)
            pool.wait_ge(zeroed, 2)
            pool.affine_select(out=mask[:, :], in_=mask[:, :], compare_op=ALU.is_ge, fill=0.0, base=0,
                               pattern=[[-HD, HC]], channel_multiplier=1).then_inc(zeroed, 1)
            pool.wait_ge(zeroed, 3)
            pool.affine_select(out=mask[:, :], in_=mask[:, :], compare_op=ALU.is_ge, fill=0.0, base=HD - 1,
                               pattern=[[HD, HC]], channel_multiplier=-1).then_inc(consts, 1)
            pool.memset(before[:, :], 1.0).then_inc(zeroed, 1)
            pool.wait_ge(zeroed, 4)
            pool.affine_select(out=before[:, :], in_=before[:, :], compare_op=ALU.is_gt, fill=0.0, base=0,
                               pattern=[[1, 128]], channel_multiplier=-1).then_inc(consts, 1)
            for tile, pattern, base, row_step in (
                    (nobody[:, :, :, 0], [[SLOTS, 2 * E], [1, SLOTS // 128]], 2 * T, SLOTS // 128),
                    (eid[:, :, :], [[0, J], [1, E]], 0, 0), (start[0][:, 0, :], [[REGION, E]], 0, 0),
                    (grid[:, :, :], [[0, E], [SLOTS, MOST]], 0, 0),
                    (tnum[:, :, :], [[1, NT], [0, E]], 0, 0)):
                pool.iota(tile, pattern=pattern, base=base, channel_multiplier=row_step,
                          allow_small_or_imprecise_dtypes=True).then_inc(consts, 1)

            pool.wait_ge(ones_set, 4)
            for i in range(2):
                v = vbd[i][:, :, :, :, :].rearrange("p t a g v -> p (t a g) v")[:, :, 32:34]
                pool.affine_select(out=v, in_=v, compare_op=ALU.not_equal, fill=0.0, base=-(SL - 1),
                                   pattern=[[0, v.shape[1]], [0, 2]], channel_multiplier=1).then_inc(zeroed, 1)
                pool.wait_ge(zeroed, 5 + i)
                last = pool.affine_select(out=v, in_=v, compare_op=ALU.not_equal, fill=0.0, base=-(2 * SL - 1),
                                          pattern=[[0, v.shape[1]], [0, 2]], channel_multiplier=1)
            last.then_inc(consts, 1)

            def rsqrt(b, mv_, var_, rstd_, got, plus, done):
                pool.wait_ge(got, b + 1)
                pool.tensor_tensor(var_[:, :], mv_[:, :, 1], eps[:, :], ALU.add).then_inc(plus, 1)
                pool.wait_ge(plus, b + 1)
                pool.tensor_tensor(rstd_[:, :], var_[:, :], mhalf[:, :], ALU.pow).then_inc(done, 1)

            def apply(to, of, mv_, rstd_):
                pool.sem_inc(applied, 1)
                for t in range(2):
                    last = pool.tensor_scalar(to[:, t, 0:CH], of[:, t, :], mv_[:, t, 0:1], rstd_[:, t:t + 1], ALU.subtract, ALU.mult)
                return last

            def step(k, c):
                s = 4 * k + c
                if is_image(k, c + 2):
                    rsqrt(s + 2, mv, vare, rstd, ln_mv, ln_var, ln_rstd)
                    wait(pool, xT_mm, s + 2)
                    pool.wait_ge(ln_rstd, s + 3)
                    apply(xn, h[(c + 2) % 4], mv, rstd).then_inc(xn_ready, 1)
                if is_image(k, c - 1):
                    rsqrt(s - 1, mv2, vare2, rstd2, ln2_mv, ln2_var, ln2_rstd)
                    wait(pool, x2_st[(c - 1) % 4], 16 * (k + (c - 1) // 4))
                    wait(pool, sent[(c - 1) % 4], 64 * (k + (c - 1) // 4))
                    pool.wait_ge(ln2_rstd, s)
                    apply(x2[(c - 1) % 4], h1[(c - 1) % 2], mv2, rstd2)
                    number = x2[(c - 1) % 4][:, :, CH]
                    if isinstance(k, int) and 4 * k + c - 1 == 0:
                        pool.iota(number, pattern=[[2, J]], base=0, channel_multiplier=2 * J,
                                  allow_small_or_imprecise_dtypes=True).then_inc(x2_ready, 1)
                    else:
                        pool.wait_ge(x2_ready, s - 1)
                        pool.tensor_tensor(number, x2[(c - 2) % 4][:, :, CH], per_image[:, :], ALU.add).then_inc(x2_ready, 1)
                if is_image(k, c - 3):
                    i = (c - 3) % 4
                    pool.wait_ge(x2_ready, s - 2)
                    pool.wait_ge(pos_ready, s - 2)
                    pool.sem_inc(images_sent, 1)
                    for n in range(2):
                        for t in range(J):
                            pool.indirect_dma_start(slots, bass.IndirectOffsetOnAxis(ap=posi[i % 2][:, n, t:t + 1], axis=0),
                                                    x2[i][:, t, :], None).then_inc(sent[i], 16)
            steps(pool, step)
            for i in range(4):
                pool.wait_ge(sent[i], 64 * (B // 4))

        @block.tensor
        def _(pe):
            pe.wait_ge(consts, CONSTS)
            pe.wait_ge(const_in, 80)

            def step(k, c):
                s = 4 * k + c
                two, nxt, cur, prev = (is_image(k, c + i) for i in (2, 1, 0, -1))

                def transpose_probs(t):
                    pe.wait_ge(exp_done, 2 * s + 1 + t)
                    wait(pe, av_ev, 2 * s + t)
                    for pr in range(PAIRS):
                        last = pe.transpose(pyz[:, pr, :], prob[t][:, 2 * pr:2 * pr + 2, :].rearrange("p h k -> p (h k)"),
                                            ident[:, :])
                    last.then_inc(pt_mm, 1)

                def weigh_values(t):
                    pe.wait_ge(pt_ev, 2 * s + 1 + t)
                    pe.wait_ge(v_ev, s + 1)
                    for pr in range(PAIRS):
                        last = pe.matmul(pyz[:, pr, 0:2 * VW], pT[t][:, pr, :],
                                         vbd[c % 2][:, t, pr, :, :].rearrange("p g v -> p (g v)"), start=True, stop=True)
                    last.then_inc(av_mm, 1)

                def scores(t):
                    wait(pe, sub_done, 2 * s + 1 + t)
                    for cc in range(2):
                        for gg in range(2):
                            g = 2 * t + gg
                            last = pe.matmul(sc[t][SL * gg:SL * gg + SL, cc, 0:HC * SL],
                                             qT[:, cc, g * SL:(g + 1) * SL],
                                             kbd[:, cc * GROUPS + g, :, :].rearrange("p h k -> p (h k)"),
                                             start=True, stop=True)
                    last.then_inc(s_mm, 1)

                if nxt:
                    pe.wait_ge(xT_ev, s + 2)
                    for m in range(2):
                        for cc in range(2):
                            last = pe.matmul(k_v[:, m * 256:(m + 1) * 256], wqkv[:, cc, CH + m * KC:CH + (m + 1) * KC],
                                             xT[:, cc, :, :].rearrange("p g n -> p (g n)"), start=(cc == 0), stop=(cc == 1))
                    last.then_inc(k_mm, 1)
                if cur:
                    transpose_probs(0)
                if is_image(k, c - 2):
                    pe.wait_ge(x2_ready, s - 1)
                    wait(pe, sub_done, 2 * s + 1 if cur else 0)
                    pe.wait_ge(sub_done, 2 * B if not cur else 1)
                    for cc in range(2):
                        for t in range(2):
                            last = pe.transpose(x2t_v[:, cc, t * HT:(t + 1) * HT], x2[(c - 2) % 4][:, t, cc * KC:(cc + 1) * KC],
                                                ident[0:HT, 0:HT])
                    last.then_inc(x2_tr, 1)
                if is_image(k, c - 3):
                    pe.wait_ge(mask_ready, s - 2)
                    if cur:
                        pe.wait_ge(sub_done, 2 * s + 2)
                    wait(pe, summed, s - 3)
                    m = mask2[(c - 3) % 2][:, :, :].rearrange("p j e -> p (j e)")
                    pe.matmul(sc[1][:, 1, 0:J * E], before[:, :], m, start=True, stop=True)
                    pe.matmul(sc[1][:, 1, J * E:2 * J * E], ones[:, :], m, start=True, stop=True).then_inc(rk_mm, 1)
                if prev:
                    pe.wait_ge(aux_ready, s)
                    pe.wait_ge(ot_ev, s)
                    for t in range(2):
                        pe.matmul(pr_v[:, t, :], oT[:, 0, t * HT:(t + 1) * HT], wproj[:, 0, :], start=True, stop=False)
                        last = pe.matmul(pr_v[:, t, :], oT[0:KC, 1, t * HT:(t + 1) * HT], wproj[0:KC, 1, :],
                                         start=False, stop=True)
                    last.then_inc(proj_mm, 1)
                if cur:
                    weigh_values(0)
                if is_image(k, c - 2):
                    pe.wait_ge(x2T_ev, s - 1)
                    if cur:
                        pe.wait_ge(sub_done, 2 * s + 2)
                    for t in range(2):
                        for cc in range(2):
                            last = pe.matmul(lg_v[:, t * E:(t + 1) * E], x2T[:, cc, t * HT:(t + 1) * HT], rt[:, cc, :],
                                             start=(cc == 0), stop=(cc == 1))
                    last.then_inc(lg_mm, 1)
                if nxt:
                    wait(pe, h1_ready, s)
                    wait(pe, ot_ev, s)
                    for m in range(2):
                        for cc in range(2):
                            last = pe.matmul(q_v[:, m * 256:(m + 1) * 256], wqkv[:, cc, m * KC:(m + 1) * KC],
                                             xT[:, cc, :, :].rearrange("p g n -> p (g n)"), start=(cc == 0), stop=(cc == 1))
                    last.then_inc(q_mm, 1)
                    pe.wait_ge(k_ev, s + 2)
                    for t in range(2):
                        for cc in range(2):
                            last = pe.matmul(v_v[:, t, :], xT[:, cc, 2 * t:2 * t + 2, :].rearrange("p g n -> p (g n)"),
                                             wqkv[:, cc, 2 * CH:3 * CH], start=(cc == 0), stop=(cc == 1))
                    last.then_inc(v_mm, 1)
                if cur:
                    transpose_probs(1)
                if nxt:
                    pe.wait_ge(kbd_ready, s + 2)
                    pe.wait_ge(k_ev, s + 2)
                    pe.wait_ge(q_ev, s + 2)
                    wait(pe, x2T_ev, s - 1)
                    scores(0)
                if cur:
                    weigh_values(1)
                if two:
                    pe.wait_ge(xn_ready, s + 3)
                    wait(pe, v_ev, s + 2)
                    for cc in range(2):
                        for t in range(2):
                            last = pe.transpose(x_v[:, cc, t * HT:(t + 1) * HT], xn[:, t, cc * KC:(cc + 1) * KC],
                                                ident[0:HT, 0:HT])
                    last.then_inc(xT_mm, 1)
                if nxt:
                    wait(pe, exp_ev, s - 1)
                    wait(pe, summed, s - 2)
                    scores(1)
                if cur:
                    pe.wait_ge(av_ev, 2 * s + 2)
                    pe.wait_ge(q_ev, s + 1)
                    for cc in range(2):
                        for t in range(2):
                            last = pe.transpose(ot_v[:, cc, t * 128:(t + 1) * 128], o[:, t, cc * KC:(cc + 1) * KC], ident[:, :])
                    last.then_inc(ot_mm, 1)
            steps(pe, step)

        @block.scalar
        def _(act):
            act.wait_ge(consts, CONSTS)
            for e in range(E):
                zero_rows(act, E * REGION + e * SLOTS, E + e, tail_st)

            def step(k, c):
                s = 4 * k + c
                two, nxt, cur = (is_image(k, c + i) for i in (2, 1, 0))

                def copy_probs(t):
                    act.wait_ge(pt_mm, 2 * s + 1 + t)
                    wait(act, av_mm, 2 * s - 1 + t)
                    act.activation(pT[t][:, :, :], pyz[:, 0:PAIRS, :], ACT.Copy).then_inc(pt_ev, 1)

                def exponentials(i, t):
                    act.wait_ge(sub_done, 2 * i + 1 + t)
                    act.activation(prob[t][:, :, 0:KEYS], prob[t][:, :, 0:KEYS], ACT.Exp, scale=float(HD) ** -0.5)\
                       .then_inc(exp_done, 1)

                if nxt:
                    act.wait_ge(k_mm, s + 2)
                    wait(act, kbd_ready, s + 1)
                    act.activation(kT[:, :, :].rearrange("p c n -> p (c n)"), k_v, ACT.Copy).then_inc(kT_ready, 1)
                if cur:
                    exponentials(s, 1)
                    copy_probs(0)
                if is_image(k, c - 2):
                    act.wait_ge(x2_tr, s - 1)
                    wait(act, lg_mm, s - 2)
                    act.activation(x2T[:, :, :], x2t_v, ACT.Copy).then_inc(x2T_ev, 1)
                if nxt:
                    wait(act, s_mm, 2 * s + 2)
                    for hd in range(HC // 2, HC):
                        last = act.activation(kbd[:, :, hd, :], k_v.rearrange("p (g k) -> p g k", k=SL), ACT.Copy, scale=mask[:, hd:hd + 1])
                    last.then_inc(k_ev, 1)
                if is_image(k, c - 2):
                    act.wait_ge(lg_mm, s - 1)
                    wait(act, route, ROUTE * (s - 2))
                    act.activation(expo[:, :, :].rearrange("p j e -> p (j e)"), lg_v, ACT.Exp, scale=-1.0).then_inc(exp_ev, 1)
                if nxt:
                    act.wait_ge(q_mm, s + 2)
                    wait(act, s_mm, 2 * s + 2)
                    act.activation(qT[:, :, :].rearrange("p c n -> p (c n)"), q_v, ACT.Copy).then_inc(q_ev, 1)
                    act.wait_ge(v_mm, s + 2)
                    wait(act, av_mm, 2 * s)
                    for gg in range(2):
                        for hh in range(2):
                            src = v_v[64 * gg:64 * gg + 64, :, :].rearrange("p t (a h d) -> p t a h d", h=2, d=HD)[:, :, :, hh, :]
                            dst = vbd[(c + 1) % 2][64 * hh:64 * hh + 64, :, :, gg, hh * HD:(hh + 1) * HD]
                            last = act.activation(dst, src, ACT.Copy)
                    last.then_inc(v_ev, 1)
                if cur:
                    copy_probs(1)
                if two:
                    act.wait_ge(xT_mm, s + 3)
                    wait(act, v_mm, s + 2)
                    for cc in range(2):
                        for t in range(2):
                            col = x_v[:, cc, t * HT:(t + 1) * HT]
                            act.activation(xT[:, cc, t::2, AUX:KEYS], col[:, AUX // 2:HT].rearrange("p (i g) -> p g i", g=GROUPS // 2),
                                           ACT.Copy)
                            a = col[:, 0:AUX // 2].rearrange("p (o a) -> p o a", o=1).to_broadcast([KC, GROUPS, AUX // 2])
                            last = act.activation(xT[:, cc, :, t:AUX:2], a, ACT.Copy)
                    last.then_inc(xT_ev, 1)
                if nxt:
                    exponentials(s + 1, 0)
                if cur:
                    act.wait_ge(ot_mm, s + 1)
                    wait(act, proj_mm, s)
                    wait(act, aux_ready, s)
                    for cc in range(2):
                        slot = ot_v[:, cc, :].rearrange("p (g n) -> p g n", n=SL)
                        for t in range(2):
                            col = oT[0:KC, cc, t * HT + AUX // 2:(t + 1) * HT]
                            act.activation(col.rearrange("p (i g) -> p g i", g=GROUPS // 2), slot[:, t::2, AUX:KEYS], ACT.Copy)
                        last = act.activation(auxp[:, cc, :, :], slot[:, :, 0:AUX], ACT.Copy)
                    last.then_inc(ot_ev, 1)
            steps(act, step)
            pad(act, range(1, E, 2))

        @block.vector
        def _(dve):
            for tile, value in ((ones[:, :], 1.0), (zrow[:, :, :], 0.0), (zeros_e[:, :], 0.0)):
                dve.memset(tile, value).then_inc(consts, 1)
            dve.memset(oT[KC:KC + 1, :, :], 1.0).then_inc(consts, 1)
            dve.memset(xT[:, :, :, :], 0.0).then_inc(consts, 1)
            for t in range(2):
                dve.memset(prob[t][:, :, :], 0.0).then_inc(consts, 1)
            for i in range(2):
                last = dve.memset(vbd[i][:, :, :, :, :], 0.0)
            last.then_inc(values_zeroed, 1)
            dve.wait_ge(values_zeroed, 1)
            for i in range(2):
                for hh in range(2):
                    dve.memset(vbd[i][64 * hh:64 * hh + 64, :, :, :, 32 + hh], 1.0).then_inc(ones_set, 1)
            dve.wait_ge(consts, CONSTS)
            dve.wait_ge(const_in, 80)

            def chain(sem_, before_):
                done = [0]

                def then(instruction):
                    done[0] += 1
                    instruction.then_inc(sem_, 1)
                    dve.wait_ge(sem_, before_ + done[0])
                return then

            def over_k(a):
                return a.rearrange("p (o j) e -> p o j e", o=1).to_broadcast([HT, 2, J, E])

            def choose(k, c):
                b, i = 4 * k + c, c % 2
                dve.wait_ge(exp_ev, b + 1)
                then = chain(route, ROUTE * b)
                then(dve.tensor_scalar(expo[:, :, :], expo[:, :, :], 1.0, None, ALU.add))
                then(dve.reciprocal(sig[:, :, :], expo[:, :, :]))
                then(dve.tensor_tensor(sel[:, :, :], sig[:, :, :],
                                       bal[:, :].rearrange("p (o e) -> p o e", o=1).to_broadcast([HT, J, E]), ALU.add))
                dve.memset(carrier[:, :], 0.0)
                for j in range(J):
                    last = dve.max(top[:, j, :], sel[:, j, :])
                then(last)
                dve.memset(carrier[:, :], 0.0)
                for j in range(J):
                    last = dve.max_index(topi[:, j, :], top[:, j, :], sel[:, j, :])
                then(last)
                dve.tensor_copy(x2[c % 4][:, :, CH + 1], topi[:, :, 0])
                wait(dve, pos_ready, b - 1)
                for n in range(2):
                    last = dve.tensor_tensor(pick[i][:, n, :, :], topi[:, :, n:n + 1].to_broadcast([HT, J, E]), eid[0:HT, :, :],
                                             ALU.is_equal)
                then(last)
                wait(dve, rk_mm, b - 1)
                dve.tensor_tensor(mask2[i][:, :, :], pick[i][:, 0, :, :], pick[i][:, 1, :, :], ALU.add).then_inc(mask_ready, 1)
                then(dve.tensor_tensor(prod[:, :, :, :], pick[i][:, :, :, :], over_k(sig[:, :, :]), ALU.mult))
                then(dve.tensor_reduce(chosen[:, :, :], prod[:, :, :, :], AXX, ALU.add))
                then(dve.tensor_tensor(wsum[:, :], chosen[:, 0, :], chosen[:, 1, :], ALU.add))
                then(dve.tensor_scalar(wsum[:, :], wsum[:, :], 1e-20, None, ALU.add))
                then(dve.reciprocal(wsum[:, :], wsum[:, :]))
                wait(dve, meta_st[c % 4], 16 * (k + c // 4))
                dve.tensor_tensor(meta[c % 4][:, 2:4, :], chosen[:, :, :],
                                  wsum[:, :].rearrange("p (o j) -> p o j", o=1).to_broadcast([HT, 2, J]), ALU.mult)\
                   .then_inc(weight_ready, 1)

            def find_rows(k, c):
                b, i = 4 * k + c, c % 2
                dve.wait_ge(rk_mm, b + 1)
                then = chain(place, PLACE * b)
                then(dve.tensor_tensor(start[i][:, 1, :], start[i][:, 0, :], total_v[:, 0, :], ALU.add))
                then(dve.tensor_tensor(start[1 - i][:, 0, :], start[i][:, 1, :], total_v[:, 1, :], ALU.add))
                then(dve.tensor_tensor(rows[:, :, :], rank_v, start[i][0:HT, :, :], ALU.add))
                then(dve.tensor_tensor(prod2[:, :, :, :], pick[i][:, :, :, :], over_k(rows[:, :, :]), ALU.mult))
                dve.wait_ge(weight_ready, b + 1)
                dve.tensor_reduce(meta[c % 4][:, 0:2, :], prod2[:, :, :, :], AXX, ALU.add).then_inc(summed, 1)
                wait(dve, sent[(c - 2) % 4], 64 * (k + (c - 2) // 4 + 1))
                dve.wait_ge(summed, b + 1)
                dve.tensor_copy(posi[i][:, :, :], meta[c % 4][:, 0:2, :]).then_inc(pos_ready, 1)

            def step(k, c):
                s = 4 * k + c
                nxt, cur, prev, two = is_image(k, c + 1), is_image(k, c), is_image(k, c - 1), is_image(k, c + 2)

                def normalise(t):
                    dve.wait_ge(av_mm, 2 * s + 1 + t)
                    for gg in range(2):
                        rows = slice(64 * gg, 64 * gg + 64)
                        last = dve.reciprocal(rden[rows, t, :, :], pyz[rows, 0:PAIRS, gg * VW + 32:gg * VW + 34])
                    last.then_inc(rden_ready, 1)
                    wait(dve, ot_mm, s)
                    dve.wait_ge(rden_ready, 2 * s + 1 + t)
                    for gg in range(2):
                        rows = slice(64 * gg, 64 * gg + 64)
                        last = dve.tensor_tensor(
                            o[rows, t, :].rearrange("p (a h d) -> p a h d", h=2, d=HD),
                            pyz[rows, 0:PAIRS, gg * VW:gg * VW + 32].rearrange("p a (h d) -> p a h d", d=HD),
                            rden[rows, t, :, :].rearrange("p a (h o) -> p a h o", o=1).to_broadcast([64, PAIRS, 2, HD]), ALU.mult)
                    last.then_inc(av_ev, 1)

                def subtract_max(t):
                    dve.wait_ge(s_mm, 2 * s + 3 + t)
                    v = sc[t][:, :, 0:HC * SL].rearrange("p c (h k) -> p c h k", k=SL)[:, :, :, 0:KEYS]
                    dve.tensor_reduce(rmax[:, t, :].rearrange("p (c h) -> p c h", c=2), v, AXX, ALU.max).then_inc(rmax_ready, 1)
                    dve.wait_ge(rmax_ready, 2 * s + 3 + t)
                    wait(dve, pt_mm, 2 * s + 1 + t)
                    dve.tensor_tensor(prob[t][:, :, 0:KEYS].rearrange("p (c h) k -> p c h k", c=2), v,
                                      rmax[:, t, :].rearrange("p (c h o) -> p c h o", c=2, o=1).to_broadcast([128, 2, HC, KEYS]),
                                      ALU.subtract).then_inc(sub_done, 1)

                if two:
                    wait(dve, xn_ready, s + 2)
                    dve.wait_ge(h_in[(c + 2) % 4], 32 * (k + (c + 2) // 4 + 1))
                    for t in range(2):
                        last = dve.bn_stats(stats[:, t, :], h[(c + 2) % 4][:, t, :])
                    last.then_inc(ln_stats, 1)
                    dve.wait_ge(ln_stats, s + 3)
                    dve.memset(carrier[:, :], 0.0)
                    for t in range(2):
                        last = dve.bn_aggr(mv[:, t, :], stats[:, t, :])
                    last.then_inc(ln_mv, 1)
                if prev:
                    dve.wait_ge(proj_mm, s)
                    wait(dve, h1_st[(c - 1) % 2], 16 * (2 * k + (c - 1) // 2))
                    dve.tensor_tensor(h1[(c - 1) % 2][:, :, :], pr_v, h[(c - 1) % 4][:, :, :], ALU.add).then_inc(h1_ready, 1)
                if nxt:
                    dve.wait_ge(kT_ready, s + 2)
                    wait(dve, s_mm, 2 * s + 2)
                    for hd in range(HC // 2):
                        last = dve.tensor_scalar(kbd[:, :, hd, :], kT[:, :, :], mask[:, hd:hd + 1], None, ALU.mult)
                    last.then_inc(kbd_ready, 1)
                if cur:
                    normalise(0)
                if prev:
                    wait(dve, x2_ready, s - 1)
                    dve.wait_ge(h1_ready, s)
                    for t in range(2):
                        last = dve.bn_stats(stats2[:, t, :], h1[(c - 1) % 2][:, t, :])
                    last.then_inc(ln2_stats, 1)
                    dve.wait_ge(ln2_stats, s)
                    dve.memset(carrier[:, :], 0.0)
                    for t in range(2):
                        last = dve.bn_aggr(mv2[:, t, :], stats2[:, t, :])
                    last.then_inc(ln2_mv, 1)
                if is_image(k, c - 3):
                    find_rows(k, c - 3)
                if is_image(k, c - 2):
                    choose(k, c - 2)
                if cur:
                    normalise(1)
                if nxt:
                    subtract_max(0)
                    subtract_max(1)
                if cur:
                    dve.wait_ge(ot_ev, s + 1)
                    dve.tensor_reduce(auxs[:, :, :], auxp[:, :, :, :].rearrange("p c g a -> p c a g"), AXX, ALU.add).then_inc(aux_sum, 1)
                    dve.wait_ge(aux_sum, s + 1)
                    for t in range(2):
                        last = dve.tensor_scalar(oT[0:KC, :, t * HT:t * HT + AUX // 2], auxs[:, :, t::2], 1.0 / GROUPS, None, ALU.mult)
                    last.then_inc(aux_ready, 1)
            steps(dve, step)

            final = start[B % 2]
            then = chain(plan, 0)
            dve.tensor_copy(last_row[:, :], final[0:1, 0, :]).then_inc(pad_ready, 1)
            then(dve.scalar_tensor_tensor(count[:, :], eid[:, 0, :], -float(REGION), final[:, 0, :], ALU.mult, ALU.add))
            then(dve.tensor_tensor(over[:, :, :], count[:, :].rearrange("o (e j) -> o e j", j=1).to_broadcast([128, E, MOST]),
                                   grid[:, :, :], ALU.is_gt))
            then(dve.tensor_reduce(ntile[:, :], over[:, :, :], AXX, ALU.add))
            then(dve.tensor_tensor_scan(ends[:, :], ntile[:, :], zeros_e[:, :], 0.0, ALU.add, ALU.add))
            then(dve.tensor_scalar(step_e[:, :], ntile[:, :], -float(SLOTS), float(REGION), ALU.mult, ALU.add))
            wide = lambda a: a.rearrange("o (t e) -> o t e", t=1).to_broadcast([128, NT, E])
            then(dve.tensor_tensor(past[:, :, :], tnum[:, :, :], wide(ends[:, :]), ALU.is_ge))
            then(dve.tensor_tensor(skip[:, :, :], past[:, :, :], wide(step_e[:, :]), ALU.mult))
            then(dve.tensor_reduce(tbase[:, :], skip[:, :, :], AXX, ALU.add))
            then(dve.tensor_reduce(texp[:, :], past[:, :, :], AXX, ALU.add))
            then(dve.scalar_tensor_tensor(tbase[:, :], tnum[:, :, 0], float(SLOTS), tbase[:, :], ALU.mult, ALU.add))
            then(dve.tensor_scalar(texp[:, :], texp[:, :], float(E - 1), None, ALU.min))
            dve.tensor_copy(tile_i[:, 0, :], tbase[0:1, :])
            dve.tensor_copy(tile_i[:, 1, :], texp[0:1, :])


def routed_experts(nc, slots, tile_i, texp, w_experts, y_rows):
    NT, E = tile_i.shape[2], w_experts.shape[0]
    R, I = 4, SLOTS // 128
    I32 = mybir.dt.int32
    rows_max = slots.shape[0] - SLOTS
    with ExitStack() as ctx:
        sb = lambda name, shape, dt=F32: ctx.enter_context(nc.sbuf_tensor(name, shape, dt))
        sem = lambda name: ctx.enter_context(nc.semaphore(name))
        pb = lambda name, shape: ctx.enter_context(nc.psum_tensor(name, shape, F32))
        ident = sb("ident_x", [128, 128])
        x = [sb(f"x_x{i}", [128, I, ROW]) for i in range(R)]
        dest = [sb(f"dest{i}", [128, I]) for i in range(R)]
        dest_i = [sb(f"dest_i{i}", [128, I], I32) for i in range(R)]
        w = [sb(f"w_x{i}", [KC, 2, 2, CH]) for i in range(R)]
        xT_high = [sb(f"xT_high_x{i}", [KC, 2, SLOTS], F32R) for i in range(2)]
        xT_low = [sb(f"xT_low_x{i}", [KC, 2, SLOTS], F32R) for i in range(2)]
        w_high = [sb(f"w_high_x{i}", [KC, 2, CH], F32R) for i in range(2)]
        w_low = [sb(f"w_low_x{i}", [KC, 2, CH], F32R) for i in range(2)]
        relu = [sb(f"relu_x{i}", [KC, 2, SLOTS]) for i in range(2)]
        hT = [sb(f"hT_x{i}", [KC, 2, SLOTS]) for i in range(2)]
        y = [sb(f"y_x{i}", [128, I, CH]) for i in range(R)]
        tp = [pb(f"tp_x{i}", [128, 2, SLOTS]) for i in range(2)]
        hp = [pb(f"hp_x{i}", [128, 2, SLOTS]) for i in range(2)]
        yp = [pb(f"yp_x{i}", [128, I, 256]) for i in range(2)]
        zeroed, consts = sem("zeroed_x"), sem("consts_x")
        x_in = [sem(f"x_in_x{i}") for i in range(R)]
        w_in = [sem(f"w_in_x{i}") for i in range(R)]
        y_st = [sem(f"y_st{i}") for i in range(R)]
        dest_ready, tiles_begun = sem("dest_ready"), sem("tiles_begun")
        x_tr, x_high, x_parts, w_high_done, w_parts, up_mm, relu_ev, sq_done, dn_mm, y_ev = (
            sem(n) for n in ("x_tr_x", "x_high_x", "x_parts_x", "w_high_done", "w_parts_x", "up_mm_x", "relu_ev_x", "sq_done_x", "dn_mm_x", "y_ev"))
        block = ctx.enter_context(nc.Block())

        def steps(eng, step, first=-2):
            whole = (NT - 6) // R
            for c in range(first, 2 + R):
                step(0, c)
            with eng.Fori(1, whole) as k:
                for c in range(2, 2 + R):
                    step(k, c)
            for t in range(R * whole + 2, NT):
                step(whole, t - R * whole)

        LAST = (NT - 1) // R, (NT - 1) % R

        def is_tile(k, c):
            return not isinstance(k, int) or 0 <= R * k + c < NT

        @block.gpsimd
        def _(pool):
            make_identity(nc, ident[:, :], 128, zeroed, consts)

            def send(k, c):
                pool.wait_ge(y_ev, R * k + c + 1)
                pool.sem_inc(tiles_begun, 1)
                for n in range(I):
                    pool.indirect_dma_start(y_rows, bass.IndirectOffsetOnAxis(ap=dest_i[c % R][:, n:n + 1], axis=0),
                                            y[c % R][:, n, :], None).then_inc(y_st[c % R], 16)

            def step(k, c):
                if is_tile(k, c - 1):
                    send(k, c - 1)
            steps(pool, step)
            send(*LAST)
            for i in range(R):
                pool.wait_ge(y_st[i], 16 * I * ((NT + R - 1 - i) // R))

        @block.sync
        def _(sp):
            def load(k, c):
                t, i = R * k + c, c % R
                row = sp.value_load(tile_i[0:1, 0, bass.ds(t, 1)], min_val=0, max_val=rows_max)
                e = sp.value_load(tile_i[0:1, 1, bass.ds(t, 1)], min_val=0, max_val=E - 1)
                wait(sp, x_tr, t + 1 - R)
                wait(sp, dest_ready, t + 1 - R)
                sp.dma_start(x[i][:, :, :], slots[bass.ds(row, SLOTS), :].rearrange("(p i) c -> p i c", i=I)).then_inc(x_in[i], 16)
                wait(sp, dn_mm, t + 1 - R)
                sp.dma_start(w[i][:, :, :, :], w_experts[bass.ds(e, 1), :, :, :, :].rearrange("o p w k n -> (o p) w k n"))\
                    .then_inc(w_in[i], 16)
            for c in range(R):
                load(0, c)

            def step(k, c):
                if is_tile(k, c + R):
                    load(k, c + R)
            steps(sp, step, first=0)

        @block.tensor
        def _(pe):
            pe.wait_ge(consts, 1)

            def step(k, c):
                t = R * k + c
                if is_tile(k, c + 2):
                    i = (c + 2) % R
                    pe.wait_ge(x_in[i], 16 * (k + (c + 2) // R + 1))
                    wait(pe, x_parts, t + 1)
                    for cc in range(2):
                        for n in range(I):
                            last = pe.transpose(tp[c % 2][0:KC, cc, n * 128:(n + 1) * 128], x[i][:, n, cc * KC:(cc + 1) * KC], ident[:, :])
                    last.then_inc(x_tr, 1)
                if is_tile(k, c + 1):
                    i = (c + 1) % 2
                    pe.wait_ge(w_parts, t + 2)
                    pe.wait_ge(x_parts, t + 2)
                    wait(pe, sq_done, t)
                    for m in range(2):
                        for cc in range(2):
                            for n, (wp, xp) in enumerate(((w_high, xT_high), (w_low, xT_high), (w_high, xT_low))):
                                last = pe.matmul(hp[i][0:KC, m, :], wp[i][:, cc, m * KC:(m + 1) * KC], xp[i][:, cc, :],
                                                 start=(cc == n == 0), stop=(cc == 1 and n == 2))
                    last.then_inc(up_mm, 1)
                if is_tile(k, c):
                    pe.wait_ge(w_in[c % R], 16 * (k + c // R + 1))
                    pe.wait_ge(sq_done, t + 1)
                    wait(pe, y_ev, t - 1)
                    for n in range(I):
                        for cc in range(2):
                            last = pe.matmul(yp[c % 2][:, n, 0:CH], hT[c % 2][:, cc, n * 128:(n + 1) * 128], w[c % R][:, 1, cc, :],
                                             start=(cc == 0), stop=(cc == 1))
                    last.then_inc(dn_mm, 1)
            steps(pe, step)

        @block.vector
        def _(dve):
            def take(k, c):
                dve.wait_ge(dn_mm, R * k + c + 1)
                wait(dve, y_st[c % R], 16 * I * (k + c // R))
                dve.tensor_copy(dest_i[c % R][:, :], dest[c % R][:, :])
                dve.tensor_copy(y[c % R][:, :, :], yp[c % 2][:, :, 0:CH]).then_inc(y_ev, 1)

            def step(k, c):
                t = R * k + c
                if is_tile(k, c - 1):
                    take(k, c - 1)
                if is_tile(k, c + 2):
                    i = c % 2
                    dve.wait_ge(x_high, t + 3)
                    dve.tensor_tensor(xT_low[i][:, :, :], tp[i][0:KC, :, :], xT_high[i][:, :, :], ALU.subtract).then_inc(x_parts, 1)
                    wait(dve, y_ev, t - 1)
                    dve.scalar_tensor_tensor(dest[(c + 2) % R][:, :], x[(c + 2) % R][:, :, CH + 1], texp[:, bass.ds(t + 2, 1)],
                                             x[(c + 2) % R][:, :, CH], ALU.not_equal, ALU.add).then_inc(dest_ready, 1)
                    dve.wait_ge(w_high_done, t + 3)
                    dve.tensor_tensor(w_low[i][:, :, :], w[(c + 2) % R][:, 0, :, :], w_high[i][:, :, :], ALU.subtract)\
                       .then_inc(w_parts, 1)
                if is_tile(k, c + 1):
                    i = (c + 1) % 2
                    dve.wait_ge(relu_ev, t + 2)
                    wait(dve, dn_mm, t)
                    dve.tensor_tensor(hT[i][:, :, :], relu[i][:, :, :], hp[i][0:KC, :, :], ALU.mult).then_inc(sq_done, 1)
            steps(dve, step)
            take(*LAST)

        @block.scalar
        def _(act):
            def step(k, c):
                t = R * k + c
                if is_tile(k, c + 2):
                    act.wait_ge(x_tr, t + 3)
                    wait(act, up_mm, t + 1)
                    act.activation(xT_high[c % 2][:, :, :], tp[c % 2][0:KC, :, :], ACT.Copy).then_inc(x_high, 1)
                    act.wait_ge(w_in[(c + 2) % R], 16 * (k + (c + 2) // R + 1))
                    act.activation(w_high[c % 2][:, :, :], w[(c + 2) % R][:, 0, :, :], ACT.Copy).then_inc(w_high_done, 1)
                if is_tile(k, c + 1):
                    act.wait_ge(up_mm, t + 2)
                    wait(act, sq_done, t)
                    act.activation(relu[(c + 1) % 2][:, :, :], hp[(c + 1) % 2][0:KC, :, :], ACT.Relu).then_inc(relu_ev, 1)
            steps(act, step)


def shared_expert_and_sum(nc, x2_rows, h1_rows, w_fc, w_pr, y_rows, weights, out_rows):
    T, J = h1_rows.shape[0], 3
    UT = 128 * J
    units = T // UT
    with ExitStack() as ctx:
        sb = lambda name, shape, dt=F32: ctx.enter_context(nc.sbuf_tensor(name, shape, dt))
        sem = lambda name: ctx.enter_context(nc.semaphore(name))
        hs = [sb(f"hs_c{i}", [128, J, CH]) for i in range(4)]
        y = [sb(f"y_c{i}", [128, J, 2, CH]) for i in range(4)]
        wt = [sb(f"wt_c{i}", [128, 2, J]) for i in range(4)]
        x = [sb(f"x_c{i}", [128, J, CH]) for i in range(4)]
        ident = sb("ident_c", [128, 128])
        wup, wdn = sb("wup_s", [KC, 2, CH]), sb("wdn_s", [KC, 2, CH])
        w_high, w_low = sb("w_high_c", [KC, 2, CH], F32R), sb("w_low_c", [KC, 2, CH], F32R)
        xT_high = [sb(f"xT_high_c{i}", [KC, 2, UT], F32R) for i in range(2)]
        xT_low = [sb(f"xT_low_c{i}", [KC, 2, UT], F32R) for i in range(2)]
        relu, hT = sb("relu_c", [KC, 2, UT]), [sb(f"hT_c{i}", [KC, 2, UT]) for i in range(2)]
        pb = lambda name, shape: ctx.enter_context(nc.psum_tensor(name, shape, F32))
        tp = pb("tp_c", [128, 2, 512])
        hp = pb("hp_c", [128, 2, 512])
        yp = [pb(f"yp_c{i}", [128, 4, 256]) for i in range(2)]
        zeroed, consts, w_in = sem("zeroed_c"), sem("consts_c"), sem("w_in_c")
        x_in = [sem(f"x_in_c{i}") for i in range(4)]
        units_begun = sem("units_begun_c")
        w_high_done, w_parts = sem("w_high_done_c"), sem("w_parts_c")
        x_tr, x_high, x_parts, up_mm, relu_ev, sq_done, dn_mm, shared = (
            sem(n) for n in ("x_tr_c", "x_high_c", "x_parts_c", "up_mm_c", "relu_ev_c", "sq_done_c", "dn_mm_c", "shared_added"))
        hs_in = [sem(f"hs_in{i}") for i in range(4)]
        y_in = [sem(f"y_in{i}") for i in range(4)]
        out_st = [sem(f"out_st{i}") for i in range(4)]
        first, second = sem("first_added"), sem("second_added")
        block = ctx.enter_context(nc.Block())

        def steps(eng, step):
            for c in range(4):
                step(0, c)
            with eng.Fori(1, units // 4 - 1) as k:
                for c in range(4):
                    step(k, c)
            for c in range(4 + units % 4):
                step(units // 4 - 1, c)

        LAST = (units - 1) // 4, (units - 1) % 4

        def rows_of(a, u):
            return a[bass.ds(u * UT, UT), :].rearrange("(p j) c -> p j c", j=J)

        @block.sync
        def _(sp):
            sp.dma_start(wup[:, :, :], w_fc.rearrange("(k p) n -> p k n", p=KC)).then_inc(w_in, 16)
            sp.dma_start(wdn[:, :, :], w_pr.rearrange("(k p) n -> p k n", p=KC)).then_inc(w_in, 16)

            def step(k, c):
                u, i = 4 * k + c, c % 4
                wait(sp, second, u - 3)
                sp.dma_start(wt[i][:, :, :], weights[:, bass.ds(u * UT, UT)].rearrange("m (p j) -> p m j", j=J))\
                  .then_inc(y_in[i], 16)
                sp.dma_start(y[i][:, :, :, :], y_rows[bass.ds(2 * UT * u, 2 * UT), :].rearrange("(p j n) c -> p j n c", j=J, n=2))\
                  .then_inc(y_in[i], 16)
                wait(sp, out_st[i], 16 * (k + c // 4))
                sp.dma_start(hs[i][:, :, :], rows_of(h1_rows, u)).then_inc(hs_in[i], 16)
            steps(sp, step)

        @block.gpsimd
        def _(pool):
            make_identity(nc, ident[:, :], 128, zeroed, consts)

            def step(k, c):
                u, i = 4 * k + c, c % 4
                wait(pool, x_tr, u - 3)
                pool.sem_inc(units_begun, 1)
                pool.dma_start(x[i][:, :, :], rows_of(x2_rows, u)).then_inc(x_in[i], 16)
            steps(pool, step)

        @block.vector
        def _(dve):
            def split_x(k, c):
                dve.wait_ge(x_high, 4 * k + c + 1)
                dve.tensor_tensor(xT_low[c % 2][:, :, :], tp[0:KC, :, 0:UT], xT_high[c % 2][:, :, :], ALU.subtract)\
                   .then_inc(x_parts, 1)

            def step(k, c):
                if not isinstance(k, int) or 4 * k + c + 1 < units:
                    split_x(k, c + 1)
                if not isinstance(k, int) or 4 * k + c >= 1:
                    add(k, c - 1)

            def add(k, c):
                u, i = 4 * k + c, c % 4
                dve.wait_ge(hs_in[i], 16 * (k + c // 4) + 16)
                dve.wait_ge(dn_mm, u + 1)
                dve.tensor_tensor(hs[i][:, :, :], yp[c % 2][:, 0:J, 0:CH], hs[i][:, :, :], ALU.add).then_inc(shared, 1)
                dve.wait_ge(shared, u + 1)
                dve.wait_ge(y_in[i], 32 * (k + c // 4) + 32)
                for n, done in ((0, first), (1, second)):
                    if n:
                        dve.wait_ge(first, u + 1)
                    for j in range(J):
                        last = dve.scalar_tensor_tensor(hs[i][:, j, :], y[i][:, j, n, :], wt[i][:, n, j:j + 1], hs[i][:, j, :],
                                                        ALU.mult, ALU.add)
                    last.then_inc(done, 1)
            dve.wait_ge(w_high_done, 1)
            dve.tensor_tensor(w_low[:, :, :], wup[:, :, :], w_high[:, :, :], ALU.subtract).then_inc(w_parts, 1)
            split_x(0, 0)
            steps(dve, step)
            add(*LAST)

        @block.tensor
        def _(pe):
            pe.wait_ge(consts, 1)
            pe.wait_ge(w_in, 32)

            def transpose_x(k, c):
                u, i = 4 * k + c, c % 4
                pe.wait_ge(x_in[i], 16 * (k + c // 4) + 16)
                wait(pe, x_parts, u)
                for cc in range(2):
                    for j in range(J):
                        last = pe.transpose(tp[0:KC, cc, j * 128:(j + 1) * 128], x[i][:, j, cc * KC:(cc + 1) * KC], ident[:, :])
                last.then_inc(x_tr, 1)

            def step(k, c):
                u = 4 * k + c
                pe.wait_ge(x_parts, u + 1)
                for m in range(2):
                    wait(pe, relu_ev, 2 * u - 1 + m)
                    for cc in range(2):
                        for n, (wp, xp) in enumerate(((w_high, xT_high), (w_low, xT_high), (w_high, xT_low))):
                            last = pe.matmul(hp[0:KC, m, 0:UT], wp[:, cc, m * KC:(m + 1) * KC], xp[c % 2][:, cc, :],
                                             start=(cc == n == 0), stop=(cc == 1 and n == 2))
                    last.then_inc(up_mm, 1)
                if not isinstance(k, int) or u + 1 < units:
                    transpose_x(k, c + 1)
                if not isinstance(k, int) or u >= 1:
                    down(k, c - 1)

            def down(k, c):
                u = 4 * k + c
                wait(pe, shared, u - 1)
                pe.wait_ge(sq_done, 2 * u + 2)
                for j in range(J):
                    for cc in range(2):
                        last = pe.matmul(yp[c % 2][:, j, 0:CH], hT[c % 2][:, cc, j * 128:(j + 1) * 128], wdn[:, cc, :],
                                         start=(cc == 0), stop=(cc == 1))
                last.then_inc(dn_mm, 1)
            transpose_x(0, 0)
            pe.wait_ge(w_parts, 1)
            steps(pe, step)
            down(*LAST)

        @block.scalar
        def _(act):
            def copy_xT(k, c):
                u = 4 * k + c
                act.wait_ge(x_tr, u + 1)
                wait(act, up_mm, 2 * u - 2)
                act.activation(xT_high[c % 2][:, :, :], tp[0:KC, :, 0:UT], ACT.Copy).then_inc(x_high, 1)

            def store(k, c):
                u, i = 4 * k + c, c % 4
                act.wait_ge(second, u + 1)
                act.dma_start(rows_of(out_rows, u), hs[i][:, :, :]).then_inc(out_st[i], 16)

            def step(k, c):
                u = 4 * k + c
                for m in range(2):
                    act.wait_ge(up_mm, 2 * u + 1 + m)
                    wait(act, sq_done, 2 * u - 1 + m)
                    act.activation(relu[:, m, :], hp[0:KC, m, 0:UT], ACT.Relu).then_inc(relu_ev, 1)
                    if m == 1 and (not isinstance(k, int) or u + 1 < units):
                        copy_xT(k, c + 1)
                    wait(act, dn_mm, u - 1)
                    act.wait_ge(relu_ev, 2 * u + 1 + m)
                    act.activation(hT[c % 2][:, m, :], relu[:, m, :], ACT.Square).then_inc(sq_done, 1)
                if not isinstance(k, int) or u >= 2:
                    store(k, c - 2)
            act.wait_ge(w_in, 32)
            act.activation(w_high[:, :, :], wup[:, :, :], ACT.Copy).then_inc(w_high_done, 1)
            copy_xT(0, 0)
            steps(act, step)
            for c in range(units % 4 + 2, units % 4 + 4):
                store(units // 4 - 1, c)
            for c in range(4):
                act.wait_ge(out_st[c], 16 * ((units + 3 - c) // 4))


def program(nc, patches, w_tok, txt, w_qkv, w_proj, b_proj, w_fc, w_pr, w_experts, router_t, bias, out):
    B, N = out.shape[0], out.shape[1]
    h_img = nc.dram_tensor("h_img_dram", (patches.shape[0] * 128, CH), F32, kind="Internal").ap()
    h1 = nc.dram_tensor("h1_dram", (B * N, CH), F32, kind="Internal").ap()
    x2 = nc.dram_tensor("x2_dram", (B * N, CH), F32, kind="Internal").ap()
    T, E = B * N, router_t.shape[1]
    slot_rows = E * region_rows(T) + E * SLOTS
    tiles = -(-(2 * T + E * (SLOTS - 1)) // SLOTS)
    slots = nc.dram_tensor("slots_dram", (slot_rows, ROW), F32, kind="Internal").ap()
    y_rows = nc.dram_tensor("y_rows_dram", (2 * T + 2 * E * SLOTS + 1, CH), F32, kind="Internal").ap()
    weights = nc.dram_tensor("weights_dram", (2, T), F32, kind="Internal").ap()
    pairs = lambda a: a.rearrange("(b p t) c -> b p t c", t=2, p=N // 2)
    embed_patches(nc, patches, w_tok, h_img)
    with nc.sbuf_tensor("tile_list", [1, 2, tiles], mybir.dt.int32) as tile_list, nc.sbuf_tensor("texp", [128, tiles], F32) as texp:
        attention_and_routing(nc, h_img, txt, w_qkv, w_proj, b_proj, router_t, bias, pairs(h1), pairs(x2), slots,
                              weights.rearrange("m (b p t) -> m b p t", t=2, p=N // 2), tile_list, texp)
        routed_experts(nc, slots, tile_list, texp, w_experts, y_rows)
    shared_expert_and_sum(nc, x2, h1, w_fc, w_pr, y_rows, weights, out.rearrange("b n c -> (b n) c"))


def patch_columns(x):
    starts = np.clip(np.arange(GRID) * PATCH - OVERLAP, 0, IMG - WIN)
    idx = (starts[:, None] + np.arange(WIN)[None, :]).reshape(-1)
    B = x.shape[0]
    g = np.take(np.take(x, idx, axis=1), idx, axis=2).reshape(B, GRID, WIN, GRID, WIN, 3)
    g = g.transpose(0, 1, 3, 2, 4, 5).reshape(B * GRID * GRID // 128, 128, 12, 121)
    return np.ascontiguousarray(g.transpose(0, 3, 2, 1))


def expert_weights(w1, w2):
    w = np.stack([w1, w2], axis=1)
    return np.ascontiguousarray(w.reshape(w.shape[0], 2, 2, KC, CH).transpose(0, 3, 1, 2, 4))


def kernel(**inputs):
    import concourse.bacc as bacc
    from concourse.bass_utils import run_bass_kernel_spmd
    a = {n: np.asarray(v) for n, v in inputs.items()}
    B, n_txt = a["txt"].shape[:2]
    N = GRID * GRID + n_txt
    arrays = {
        "patches": patch_columns(a["x"]), "w_tok": a["L0_tok_W"], "txt": a["txt"],
        "w_qkv": a["L0_attn_Wqkv"], "w_proj": a["L0_attn_Wproj"], "b_proj": a["L0_attn_bproj"],
        "w_fc": a["L0_ffn_w_fc_sh"], "w_pr": a["L0_ffn_w_proj_sh"],
        "w_experts": expert_weights(a["L0_ffn_w1"], a["L0_ffn_w2"]),
        "router_t": np.ascontiguousarray(a["L0_ffn_router_w"].T), "bias": a["L0_ffn_balance_bias"],
    }
    nc = bacc.Bacc("TRN2", target_bir_lowering=False, num_devices=1)
    args = [nc.dram_tensor(n, v.shape, mybir.dt.from_np(v.dtype), kind="ExternalInput").ap() for n, v in arrays.items()]
    out = nc.dram_tensor("out_dram", (B, N, CH), F32, kind="ExternalOutput").ap()
    program(nc, *args, out)
    return run_bass_kernel_spmd(nc, [arrays], core_ids=[0]).results[0]["out_dram"]
```
